# Optimizing a Trainium2 kernel written in Bass

```python
import numpy as np
import jax
import jax.numpy as jnp

def _softmax(x, axis=-1):
    return jax.nn.softmax(x, axis=axis)

def _gelu(x):
    return jax.nn.gelu(x, approximate=True)

def _silu(x):
    return jax.nn.silu(x)

def _sigmoid(x):
    return jax.nn.sigmoid(x)

def _layernorm(x, axis=-1, eps=1e-05):
    m = jnp.mean(x, axis=axis, keepdims=True)
    v = jnp.var(x, axis=axis, keepdims=True)
    return (x - m) / jnp.sqrt(v + eps)

def _scatter_add(tgt, idx, src, axis=0):
    return tgt.at[idx].add(src)

def _segment_sum(src, seg, n):
    return jax.ops.segment_sum(src, seg, n)
kernel_name = 'mk_decoder_preln_d1_seqx_r4_0f9587'

def setup_inputs(seed: int=0):
    np.random.seed(seed)
    _w = jnp.asarray

    def _rec_inputs():
        import jax
        import jax.numpy as jnp
        _rk = jax.random.key(seed)
        x = 0.5 + 0.2887 * jax.random.normal(jax.random.fold_in(_rk, 1), (4, 512, 512), jnp.float32)
        _lenS = 512 - jax.random.randint(jax.random.fold_in(_rk, 7), (4,), 0, max(1, 512 // 4) + 1, jnp.int32)
        _lenS2 = 512 - jax.random.randint(jax.random.fold_in(_rk, 8), (4,), 0, max(1, 512 // 4) + 1, jnp.int32)
        _ctx_512P = jax.random.normal(jax.random.fold_in(_rk, 11), (4, 16, 128), jnp.float32)
        _ctx_512c = jax.random.dirichlet(jax.random.fold_in(_rk, 511), 0.3 * jnp.ones((16,), jnp.float32), (4, 512))
        _ctx_512t = jnp.einsum('bsk,bkd->bsd', _ctx_512c, _ctx_512P)
        _ctx_512t = _ctx_512t * jax.lax.rsqrt(jnp.mean(jnp.square(_ctx_512t)) + 1e-12) * 0.953939
        ctx_512 = 7.22013e-05 + 1.00017 * (_ctx_512t + 0.3 * jax.random.normal(jax.random.fold_in(_rk, 611), (4, 512, 128), jnp.float32))
        return (x, ctx_512)
    x, ctx_512 = _rec_inputs()

    def _L0_attn_setup():
        import jax, jax.numpy as jnp
        import numpy as np
        D_MODEL = 512
        N_HEADS = 16
        N_KV_HEADS = 4
        D_K = D_MODEL // N_HEADS
        KV_REP = N_HEADS // N_KV_HEADS

        def _rotate_half(u):
            u1, u2 = jnp.split(u, 2, axis=-1)
            return jnp.concatenate([-u2, u1], axis=-1)

        def _rope(q, k):
            T, d = (q.shape[2], q.shape[3])
            half = d // 2
            inv_freq = 1.0 / 10000.0 ** (jnp.arange(half, dtype=jnp.float32) / half)
            ang = jnp.arange(T, dtype=jnp.float32)[:, None] * inv_freq[None, :]
            cos = jnp.tile(jnp.cos(ang), (1, 2))[None, None]
            sin = jnp.tile(jnp.sin(ang), (1, 2))[None, None]
            q = q * cos + _rotate_half(q) * sin
            k = k * cos + _rotate_half(k) * sin
            return (q, k)
        key = jax.random.key(seed)
        ks = jax.random.split(key, 9)
        B, T = (4, 512)
        s = 0.02
        return {'x': jax.random.normal(ks[0], (B, T, D_MODEL), jnp.float32), 'wq_w': jax.random.normal(ks[1], (D_MODEL, N_HEADS * D_K), jnp.float32) * s, 'wq_b': jnp.zeros((N_HEADS * D_K,), jnp.float32), 'wk_w': jax.random.normal(ks[2], (D_MODEL, N_KV_HEADS * D_K), jnp.float32) * s, 'wk_b': jnp.zeros((N_KV_HEADS * D_K,), jnp.float32), 'wv_w': jax.random.normal(ks[3], (D_MODEL, N_KV_HEADS * D_K), jnp.float32) * s, 'wv_b': jnp.zeros((N_KV_HEADS * D_K,), jnp.float32), 'o_w': jax.random.normal(ks[4], (D_MODEL, D_MODEL), jnp.float32) * s, 'o_b': jnp.zeros((D_MODEL,), jnp.float32)}
    _L0_attn_all = _L0_attn_setup()
    _L0_attn_in = {k: v for k, v in _L0_attn_all.items() if k in ('wq_w', 'wq_b', 'wk_w', 'wk_b', 'wv_w', 'wv_b', 'o_w', 'o_b')}
    del _L0_attn_all

    def _L0_xattn_setup():
        import jax, jax.numpy as jnp
        import numpy as np
        P_ASEM = 0.6
        key = jax.random.key(seed)
        k1, k2, k3 = jax.random.split(key, 3)
        B, N, D = (8, 512, 128)
        x = jax.random.normal(k1, (B, N, D), dtype=jnp.float32)
        adj = jax.random.uniform(k2, (B, N, N), dtype=jnp.float32)
        bound = 1.0 / np.sqrt(2 * D)
        W = jax.random.uniform(k3, (1, 2 * D), dtype=jnp.float32, minval=-bound, maxval=bound)
        b = jnp.zeros((1,), dtype=jnp.float32)
        return {'x': x, 'adj': adj, 'W': W, 'b': b}
    _L0_xattn_all = _L0_xattn_setup()
    _L0_xattn_in = {k: v for k, v in _L0_xattn_all.items() if k in ('W', 'b')}
    del _L0_xattn_all

    def _L0_ffn_setup():
        import jax, jax.numpy as jnp
        import numpy as np
        from jax import lax
        TOP_K = 2
        N_EXPERTS = 8
        key = jax.random.key(seed)
        ks = jax.random.split(key, 7)
        B, S, H, I, E = (4, 512, 512, 352, N_EXPERTS)
        s_h = 1.0 / np.sqrt(H)
        s_i = 1.0 / np.sqrt(I)
        return {'hidden_states': jax.random.normal(ks[0], (B, S, H), jnp.float32), 'gate_w': jax.random.normal(ks[1], (E, H), jnp.float32) * s_h, 'w1': jax.random.normal(ks[2], (E, H, 2 * I), jnp.float32) * s_h, 'w2': jax.random.normal(ks[3], (E, I, H), jnp.float32) * s_i, 'sw1': jax.random.normal(ks[4], (I, H), jnp.float32) * s_h, 'sw2': jax.random.normal(ks[5], (I, H), jnp.float32) * s_h, 'sw3': jax.random.normal(ks[6], (H, I), jnp.float32) * s_i}
    _L0_ffn_all = _L0_ffn_setup()
    _L0_ffn_in = {k: v for k, v in _L0_ffn_all.items() if k in ('gate_w', 'w1', 'w2', 'sw1', 'sw2', 'sw3')}
    del _L0_ffn_all
    return {'x': x, 'ctx_512': ctx_512, 'L0_attn_wq_w': _L0_attn_in['wq_w'], 'L0_attn_wq_b': _L0_attn_in['wq_b'], 'L0_attn_wk_w': _L0_attn_in['wk_w'], 'L0_attn_wk_b': _L0_attn_in['wk_b'], 'L0_attn_wv_w': _L0_attn_in['wv_w'], 'L0_attn_wv_b': _L0_attn_in['wv_b'], 'L0_attn_o_w': _L0_attn_in['o_w'], 'L0_attn_o_b': _L0_attn_in['o_b'], 'L0_xattn_W': _L0_xattn_in['W'], 'L0_xattn_b': _L0_xattn_in['b'], 'L0_ffn_gate_w': _L0_ffn_in['gate_w'], 'L0_ffn_w1': _L0_ffn_in['w1'], 'L0_ffn_w2': _L0_ffn_in['w2'], 'L0_ffn_sw1': _L0_ffn_in['sw1'], 'L0_ffn_sw2': _L0_ffn_in['sw2'], 'L0_ffn_sw3': _L0_ffn_in['sw3']}

def reference(x, ctx_512, L0_attn_wq_w, L0_attn_wq_b, L0_attn_wk_w, L0_attn_wk_b, L0_attn_wv_w, L0_attn_wv_b, L0_attn_o_w, L0_attn_o_b, L0_xattn_W, L0_xattn_b, L0_ffn_gate_w, L0_ffn_w1, L0_ffn_w2, L0_ffn_sw1, L0_ffn_sw2, L0_ffn_sw3):
    import jax
    import jax.numpy as jnp

    def _L0_attn_ref(x, wq_w, wq_b, wk_w, wk_b, wv_w, wv_b, o_w, o_b):
        import jax, jax.numpy as jnp
        import numpy as np
        D_MODEL = 512
        N_HEADS = 16
        N_KV_HEADS = 4
        D_K = D_MODEL // N_HEADS
        KV_REP = N_HEADS // N_KV_HEADS

        def _rotate_half(u):
            u1, u2 = jnp.split(u, 2, axis=-1)
            return jnp.concatenate([-u2, u1], axis=-1)

        def _rope(q, k):
            T, d = (q.shape[2], q.shape[3])
            half = d // 2
            inv_freq = 1.0 / 10000.0 ** (jnp.arange(half, dtype=jnp.float32) / half)
            ang = jnp.arange(T, dtype=jnp.float32)[:, None] * inv_freq[None, :]
            cos = jnp.tile(jnp.cos(ang), (1, 2))[None, None]
            sin = jnp.tile(jnp.sin(ang), (1, 2))[None, None]
            q = q * cos + _rotate_half(q) * sin
            k = k * cos + _rotate_half(k) * sin
            return (q, k)
        B, T, _ = x.shape
        Q = (x @ wq_w + wq_b).reshape(B, T, N_HEADS, D_K).transpose(0, 2, 1, 3)
        K = (x @ wk_w + wk_b).reshape(B, T, N_KV_HEADS, D_K).transpose(0, 2, 1, 3)
        V = (x @ wv_w + wv_b).reshape(B, T, N_KV_HEADS, D_K).transpose(0, 2, 1, 3)
        Q, K = _rope(Q, K)
        K = jnp.repeat(K, KV_REP, axis=1)
        V = jnp.repeat(V, KV_REP, axis=1)
        scores = jnp.einsum('bhtd,bhTd->bhtT', Q, K)
        causal = jnp.triu(jnp.ones((T, T), bool), k=1)
        scores = jnp.where(causal, -jnp.inf, scores)
        attn = jax.nn.softmax(scores / jnp.sqrt(jnp.float32(D_K)), axis=-1)
        out = jnp.einsum('bhtT,bhTd->bhtd', attn, V)
        out = out.transpose(0, 2, 1, 3).reshape(B, T, N_HEADS * D_K)
        return out @ o_w + o_b

    def _L0_xattn_ref(x, adj, W, b):
        import jax, jax.numpy as jnp
        import numpy as np
        P_ASEM = 0.6
        D = x.shape[-1]
        Wi = W[:, :D]
        Wj = W[:, D:]
        si = jnp.einsum('bnd,d->bn', x, Wi[0])
        sj = jnp.einsum('bnd,d->bn', x, Wj[0])
        xij = jax.nn.sigmoid(si[:, :, None] + sj[:, None, :] + b[0])
        return P_ASEM * xij + (1.0 - P_ASEM) * adj

    def _L0_ffn_ref(hidden_states, gate_w, w1, w2, sw1, sw2, sw3):
        import jax, jax.numpy as jnp
        import numpy as np
        from jax import lax
        TOP_K = 2
        N_EXPERTS = 8
        B, S, H = hidden_states.shape
        x = hidden_states.reshape(-1, H)
        T = x.shape[0]
        logits = jnp.einsum('th,eh->te', x.astype(jnp.float32), gate_w.astype(jnp.float32))
        scores = jax.nn.softmax(logits, axis=-1)
        topk_w, topk_idx = lax.top_k(scores, TOP_K)
        topk_w = topk_w / (topk_w.sum(-1, keepdims=True) + 1e-20)
        topk_w = topk_w.astype(hidden_states.dtype)
        cw = jnp.zeros((T, N_EXPERTS), hidden_states.dtype).at[jnp.arange(T)[:, None], topk_idx].add(topk_w)

        def body(acc, ew):
            w1e, w2e, cwe = ew
            h = x @ w1e
            g, u = jnp.split(h, 2, axis=-1)
            y = jax.nn.silu(g) * u @ w2e
            return (acc + cwe[:, None] * y, None)
        moe, _ = lax.scan(body, jnp.zeros_like(x), (w1, w2, cw.T))
        moe = moe.reshape(B, S, H)
        shared = jnp.einsum('bsi,hi->bsh', jax.nn.silu(jnp.einsum('bsh,ih->bsi', hidden_states, sw1)) * jnp.einsum('bsh,ih->bsi', hidden_states, sw2), sw3)
        return moe + shared
    x = x + _L0_attn_ref(_layernorm(x, axis=-1), L0_attn_wq_w, L0_attn_wq_b, L0_attn_wk_w, L0_attn_wk_b, L0_attn_wv_w, L0_attn_wv_b, L0_attn_o_w, L0_attn_o_b)
    x = x + _L0_xattn_ref(ctx_512, _layernorm(x, axis=-1), L0_xattn_W, L0_xattn_b)
    x = x + _L0_ffn_ref(_layernorm(x, axis=-1), L0_ffn_gate_w, L0_ffn_w1, L0_ffn_w2, L0_ffn_sw1, L0_ffn_sw2, L0_ffn_sw3)
    return x

_drawn_inputs = setup_inputs


def setup_inputs(seed=0):
    import zlib

    import numpy as np

    out = dict(_drawn_inputs(seed))
    spreads = {'L0_attn_wq_b': (0.0, 0.59),
     'L0_attn_wk_b': (0.0, 0.8),
     'L0_attn_wv_b': (0.0, 0.1),
     'L0_attn_o_b': (0.0, 0.1)}
    factors = {}
    for name, (base, spread) in spreads.items():
        noise = np.random.default_rng([zlib.crc32(name.encode()), seed]).standard_normal(out[name].shape)
        drawn = base * np.exp(spread * noise) if base else spread * noise
        out[name] = jnp.asarray(drawn.astype(out[name].dtype))
    for name, factor in factors.items():
        out[name] = (out[name] * factor).astype(out[name].dtype)
    return out
```

```python
from contextlib import ExitStack

import concourse.bass as bass
from concourse import mybir

F32 = mybir.dt.float32
F16 = mybir.dt.float16
BF16 = mybir.dt.bfloat16
I32 = mybir.dt.int32
U32 = mybir.dt.uint32
ALU = mybir.AluOpType
ACT = mybir.ActivationFunctionType
AX = mybir.AxisListType

B, T, D = 4, 512, 512
P = 128
NT = T // P
KC = D // P
HEADS, KVH, DK = 16, 4, 32
REP = HEADS // KVH
CTX = 128
NE, FF = 8, 352
TOK = B * T
TT = TOK // P
RT = (2 * TOK + NE * (P - 1)) // P
ST = TT // 2
FCH = [(0, 128), (128, 128), (256, 96)]
W1N = KC * 2 * FF
W2N = len(FCH) * D
WN = 2 * (W1N + W2N)
WSCALE = 256.0
EPS = 1e-5
MAGIC = 0x5F3759DF
NEWTON = 13
N_LN = 2 + NEWTON
N_ROPE = 4 * 5
N_AFTER = 2 * N_LN + 2 + NT
SLAB = 3
ARENA = 9552
NPAR = 9
PAIRS = KVH * NT * 2
CHUNK = [4, 0, 1, 2, 3]
PROJ_BANK = [6, 7, 6, 7, 6]
V_BANK = [7, 6]
GROUP_BANK = [4, 6, 4, 6]
OUT_BANK = [5, 7, 5, 7]
NQKV = D + 2 * P


def wait_apart(eng, sem, value, carrier):
    eng.wait_ge(sem, value)
    if not isinstance(value, int):
        eng.sem_inc(carrier, 1)


class Chain:

    def __init__(self, eng, sem, base=0):
        self.eng, self.sem, self.base, self.n = eng, sem, base, 0

    def link(self, ins, carrier=None):
        self.n += 1
        ins.then_inc(self.sem, 1)
        if carrier is None:
            self.eng.wait_ge(self.sem, self.base + self.n)
        else:
            wait_apart(self.eng, self.sem, self.base + self.n, carrier)


def decoder_kernel(nc, x, ctx, wq, wk, wv, bqk, bv, wo, bo, wi, wj, b_x, gate, w1, w2, cosT, sinT,
                   out, h3d, xsd, x3d, disp, yd):
    x_rows = x.rearrange("b t d -> (b t) d")
    out_rows = out.rearrange("b t d -> (b t) d")
    ctx_rows = ctx.rearrange("b t d -> (b t) d")
    SC = float(DK) ** -0.5

    with ExitStack() as stack:
        def sb(name, shape, dt):
            return stack.enter_context(nc.sbuf_tensor(name, shape, dt))

        def sem(name):
            return stack.enter_context(nc.semaphore(name))

        W = sb("W", [P, (NE + 1) * WN], F16)
        ident = sb("ident", [P, P], F32)
        stage = sb("stage", [P, W1N + W2N], F32)

        arena = sb("arena", [P, ARENA], F32)
        used = {"w": SLAB * WN // 2, "a": 0}
        Wf = W[:, :].bitcast(F32)

        def take(where, n):
            o = used[where]
            used[where] = o + n
            assert used[where] <= ((NE + 1) * WN // 2 if where == "w" else ARENA), (where, used)
            return (Wf if where == "w" else arena)[:, o:o + n]

        def take16(where, n):
            return take(where, n // 2).bitcast(F16)

        wstage = stage[:, 0:KC * NQKV].rearrange("p (k n) -> p k n", k=KC)
        xb = take("w", NT * D).rearrange("p (t d) -> p t d", t=NT)
        xparts = take("w", KC * T)
        xhi = xparts[:, 0:KC * T // 2].bitcast(F16).rearrange("p (k t) -> p k t", k=KC)
        xlo = xparts[:, KC * T // 2:].bitcast(F16).rearrange("p (k t) -> p k t", k=KC)
        oT = xparts.rearrange("p (c t) -> p c t", c=KC)
        wqkv_hi = take16("w", KC * NQKV).rearrange("p (k n) -> p k n", k=KC)
        wqkv_lo = take16("w", KC * NQKV).rearrange("p (k n) -> p k n", k=KC)
        wo_sb = take("w", KC * D).rearrange("p (k n) -> p k n", k=KC)
        pT = take("w", 4 * 2 * T).rearrange("p (s h q) -> p s h q", s=4, h=2)
        cos_sb = take("w", T)
        sin_sb = take("w", T)
        th = take("w", NT * T).rearrange("p (t m) -> p t m", t=NT)
        Qst = take16("w", HEADS * T).rearrange("p (h t) -> p h t", h=HEADS)
        qk_hi = take16("w", 5 * T).rearrange("p (c t) -> p c t", c=5)
        qk_lo = take16("w", 5 * T).rearrange("p (c t) -> p c t", c=5)
        ctx_sb = take("w", NT * CTX).rearrange("p (t d) -> p t d", t=NT)
        ctxT = take("w", T)
        bo_sb = take("w", D)
        bv_sb = take("w", P)
        wj_sb = take("w", P)
        V = take("w", NT * P).rearrange("p (t d) -> p t d", t=NT)
        ones32 = take("w", DK)
        mk = take("w", P // 2).bitcast(BF16)
        identb = take("w", P // 2).bitcast(BF16)
        m = take("w", NT * HEADS).rearrange("p (t h) -> p t h", t=NT)
        bqk_sb = take("w", 6)
        wi_sb = take("w", 2)
        bx_sb = take("w", 2)
        stats = take("w", NT * 6).rearrange("p (t s) -> p t s", t=NT)
        mv = take("w", NT * 2).rearrange("p (t s) -> p t s", t=NT)
        stats2 = take("w", NT * 6).rearrange("p (t s) -> p t s", t=NT)
        mv2 = take("w", NT * 2).rearrange("p (t s) -> p t s", t=NT)
        nw = take("w", 16).rearrange("p (k t) -> p k t", k=4)
        nw2 = take("w", 16).rearrange("p (k t) -> p k t", k=4)
        sib = take("w", 4)
        lnA = take("w", 4)
        lnB = take("w", 4)
        x2 = take("a", NT * D).rearrange("p (t d) -> p t d", t=NT)
        xr = take("a", NT * D).rearrange("p (t d) -> p t d", t=NT)
        Kst = take16("a", KVH * T).rearrange("p (c t) -> p c t", c=KVH)
        qb = take("a", 2 * T).rearrange("p (s t) -> p s t", s=2)
        t1 = take("a", 2 * T).rearrange("p (s t) -> p s t", s=2)
        sh = take("a", T)
        rot = take("a", T)
        recip = rot
        Vn = sh.rearrange("p (t d) -> p t d", t=NT)
        zero = take("a", D)
        nm_hi = take16("a", T)
        nm_lo = take16("a", T)

        ps = stack.enter_context(nc.psum_tensor("ps", [P, 8, 512], F32))

        consts_ok = sem("consts_ok")
        zero_ok = sem("zero_ok")
        zeroed = sem("zeroed")
        par_in = sem("par_in")
        wqkv_in = sem("wqkv_in")
        wqkv_ok = sem("wqkv_ok")
        x_in = sem("x_in")
        ctx_ld = sem("ctx_ld")
        xr_in = sem("xr_in")
        stage_in = [sem("stage_in_w1"), sem("stage_in_w2")]
        stage_sp = [sem("stage_sp_w1"), sem("stage_sp_w2")]
        kst_in = sem("kst_in")
        qst_in = sem("qst_in")
        nm_in = sem("nm_in")
        st_out = sem("st_out")
        xn_ok = sem("xn_ok")
        xt_ok = sem("xt_ok")
        xhi_ok = sem("xhi_ok")
        xlo_ok = sem("xlo_ok")
        proj_ok = sem("proj_ok")
        qb_ok = sem("qb_ok")
        t1_ok = sem("t1_ok")
        rope_ok = sem("rope_ok")
        v_ok = sem("v_ok")
        ctxT_ps = sem("ctxT_ps")
        ctxT_ok = sem("ctxT_ok")
        si_ps = sem("si_ps")
        sib_ok = sem("sib_ok")
        sj_ps = sem("sj_ps")
        th_ok = sem("th_ok")
        pair_ok = sem("pair_ok")
        m_ok = sem("m_ok")
        mt_ps = sem("mt_ps")
        nmhi_ok = sem("nmhi_ok")
        nmlo_ok = sem("nmlo_ok")
        p_ok = sem("p_ok")
        mask_ok = sem("mask_ok")
        pv_ok = sem("pv_ok")
        oT_ok = sem("oT_ok")
        xrb_ok = sem("xrb_ok")
        op_ps = sem("op_ps")
        x2_ok = sem("x2_ok")
        x3_ok = sem("x3_ok")
        h3_ok = sem("h3_ok")
        whi_ok = sem("whi_ok")
        wlo_ok = sem("wlo_ok")
        row_in = [sem(f"row_in{i}") for i in range(B)]
        wqkv_hi_ok = sem("wqkv_hi_ok")
        rc_ok = sem("rc_ok")
        ch_ln = sem("ch_ln")
        ch_rope = sem("ch_rope")
        vc_ok = sem("vc_ok")
        ch_op = sem("ch_op")
        b_in = [sem(f"b_in{i}") for i in range(2)]
        x3_in = [sem(f"x3_in{i}") for i in range(2)]
        y_out = [sem(f"y_out{i}") for i in range(2)]
        bt_ps = sem("bt_ps")
        bhi_ok = sem("bhi_ok")
        blo_ok = sem("blo_ok")
        up_ps = sem("up_ps")
        silu_ok = sem("silu_ok")
        act_ok = sem("act_ok")
        at_ps = sem("at_ps")
        ahi_ok = sem("ahi_ok")
        alo_ok = sem("alo_ok")
        dn_ps = sem("dn_ps")
        y_ok = sem("y_ok")
        lg_ps = sem("lg_ps")
        lg_ok = sem("lg_ok")
        g_in = sem("g_in")
        g_ok = sem("g_ok")
        bconst = sem("bconst")
        e_ok = sem("e_ok")
        r_dve = sem("r_dve")
        cnt_ps = sem("cnt_ps")
        route_ok = sem("route_ok")
        sx_in = [sem("sx_in0"), sem("sx_in1")]
        sc_out = [sem("sc_out0"), sem("sc_out1")]
        gd_in = [sem("gd_in0"), sem("gd_in1")]
        ge_in = [sem("ge_in0"), sem("ge_in1")]
        xs_in = [sem("xs_in0"), sem("xs_in1")]
        fin_ok = sem("fin_ok")
        fch = sem("fch")
        fx_ok = sem("fx_ok")
        x3g_ok = sem("x3g_ok")
        fin_out = [sem("fin_out0"), sem("fin_out1")]
        pz = sem("pz")
        diff_ok = sem("diff_ok")
        kones_ok = sem("kones_ok")
        v_waits = sem("v_waits")
        pool_waits = sem("pool_waits")
        mb_ok = sem("mb_ok")
        table_ok = sem("table_ok")

        ub = {"o": 0}

        def takeb(n):
            o = ub["o"]
            ub["o"] = o + n
            assert ub["o"] <= ARENA, ub["o"]
            return arena[:, o:o + n]

        bx = takeb(2 * D).rearrange("p (s d) -> p s d", s=2)
        bhi = takeb(D).bitcast(F16).rearrange("p (s k t) -> p s k t", s=2, k=KC)
        blo = takeb(D).bitcast(F16).rearrange("p (s k t) -> p s k t", s=2, k=KC)
        sil = takeb(2 * FF).rearrange("p (s f) -> p s f", s=2)
        act = takeb(2 * FF).rearrange("p (s f) -> p s f", s=2)
        ahi = takeb(3 * P).bitcast(F16).rearrange("p (s k t) -> p s k t", s=2, k=3)
        alo = takeb(3 * P).bitcast(F16).rearrange("p (s k t) -> p s k t", s=2, k=3)
        yb = takeb(2 * D).rearrange("p (s d) -> p s d", s=2)
        x3b = takeb(2 * D).rearrange("p (s d) -> p s d", s=2)
        sx = takeb(2 * D).rearrange("p (s d) -> p s d", s=2)
        lsr = takeb(3 * TT * NE)
        LG = lsr[:, 0:TT * NE].rearrange("p (t e) -> p t e", t=TT)
        sidx = lsr[:, TT * NE:2 * TT * NE].bitcast(U32).rearrange("p (t e) -> p t e", t=TT)
        R = lsr[:, 2 * TT * NE:].rearrange("p (t e) -> p t e", t=TT)
        cmt = lsr[:, 0:RT * NE].rearrange("p (i e) -> p i e", i=RT)
        srt = takeb(TT * 8).rearrange("p (t e) -> p t e", t=TT)
        EX = takeb(TT * NE).rearrange("p (t e) -> p t e", t=TT)
        M1 = takeb(TT * NE).rearrange("p (t e) -> p t e", t=TT)
        M2 = takeb(TT * NE).rearrange("p (t e) -> p t e", t=TT)
        pre = takeb(TT * NE).rearrange("p (t e) -> p t e", t=TT)
        iota8 = takeb(TT * NE).rearrange("p (t e) -> p t e", t=TT)
        it128 = takeb(NE * 16).rearrange("p (e k) -> p e k", e=NE)
        cmp = takeb(NE * 16).rearrange("p (e k) -> p e k", e=NE)
        itile = takeb(RT * NE).rearrange("p (i e) -> p i e", i=RT)
        Mb = takeb(TT * NE // 2).bitcast(BF16)
        lt_b = takeb(P // 2).bitcast(BF16)
        on_b = takeb(P // 2).bitcast(BF16)
        idx_f = takeb(2 * TT).rearrange("p (c t) -> p c t", c=2)
        w12 = takeb(2 * TT).rearrange("p (c t) -> p c t", c=2)
        slot_f = takeb(2 * TT).rearrange("p (c t) -> p c t", c=2)
        slot_i = takeb(2 * TT).bitcast(I32).rearrange("p (c t) -> p c t", c=2)
        zs = takeb(4 * TT).rearrange("p (c t) -> p c t", c=4)
        nte = takeb(4 * NE).rearrange("p (c e) -> p c e", c=4)
        toff_f = takeb(RT + 1)
        toff = takeb(RT + 1).bitcast(I32)
        g_hi = takeb(KC * NE // 2).bitcast(F16).rearrange("p (k e) -> p k e", k=KC)
        g_lo = takeb(KC * NE // 2).bitcast(F16).rearrange("p (k e) -> p k e", k=KC)
        g_f = EX[:, 0:KC, :]
        rows16 = Wf[:, (NE - 1) * WN // 2:(NE - 1) * WN // 2 + TT * D].rearrange("p (t d) -> p t d", t=TT)
        fb0 = WN // 2
        gd = Wf[:, fb0:fb0 + 4 * D].rearrange("p (s c d) -> p s c d", s=2, c=2)
        ge = Wf[:, fb0 + 4 * D:fb0 + 8 * D].rearrange("p (s c d) -> p s c d", s=2, c=2)
        fin = stage[:, 4 * D:6 * D].rearrange("p (s d) -> p s d", s=2)
        xs = stage[:, 6 * D:8 * D].rearrange("p (s d) -> p s d", s=2)

        def static(v):
            return isinstance(v, int)

        def w_cols(off, o, n, rows_=P):
            return W[0:rows_, off + o:off + o + n] if static(off) else W[0:rows_, bass.ds(off + o, n)]

        def dram_rows(t_, base, n=P):
            return t_[base:base + n, :] if static(base) else t_[bass.ds(base, n), :]

        def pipeline(eng, base, n, step):
            loops = max(0, (n - 6) // 2) if n > ST else 0
            first = 4 if loops else 0
            for i in range(first):
                step(i, (i + base) % 2, i // 2)
            if loops:
                with eng.Fori(0, loops) as j:
                    step(j * 2 + 4, 0, j + 2)
                    step(j * 2 + 5, 1, j + 2)
            for i in range(first + 2 * loops, n + 2):
                step(i, (i + base) % 2, i // 2)

        def batches(eng, stage_fn):
            stage_fn(0)
            with eng.Fori(1, B - 2) as b:
                stage_fn(b)
            stage_fn(B - 2)
            stage_fn(B - 1)

        def has(b, ahead):
            return not static(b) or 0 <= b + ahead < B

        halves = ((0, 0, W1N, 2 * FF), (W1N, 2 * W1N, W2N, D))

        block = stack.enter_context(nc.Block())

        @block.sync
        def _(sp):
            def load_x(b):
                sp.wait_ge(xt_ok, b * NT)
                sp.dma_start(xb, dram_rows(x_rows, b * T, T).rearrange("(t p) d -> p t d", p=P)).then_inc(x_in, 16)

            def load_ctx(b):
                sp.wait_ge(ctxT_ps, b)
                sp.dma_start(ctx_sb, dram_rows(ctx_rows, b * T, T).rearrange("(t p) d -> p t d", p=P))\
                    .then_inc(ctx_ld, 16)

            def load_stacks(b):
                sp.wait_ge(pair_ok, 2 * PAIRS * b)
                sp.wait_ge(rope_ok, 5 * b + 1)
                for c in range(KVH):
                    k_hi, k_lo = qk_hi[32 * c:32 * c + 32, 4, :], qk_lo[32 * c:32 * c + 32, 4, :]
                    for at, src in ((0, k_hi), (32, k_hi), (64, k_lo)):
                        sp.dma_start(Kst[at:at + 32, c, :], src).then_inc(kst_in, 16)
                sp.wait_ge(rope_ok, 5 * b + 5)
                for r in range(REP):
                    q_hi, q_lo = qk_hi[32 * r:32 * r + 32, 0:4, :], qk_lo[32 * r:32 * r + 32, 0:4, :]
                    for at, src in ((0, q_hi), (32, q_lo), (64, q_hi)):
                        sp.dma_start(Qst[at:at + 32, r:HEADS:REP, :], src).then_inc(qst_in, 16)

            def load_negmax(b):
                sp.wait_ge(nmhi_ok, b + 1)
                sp.wait_ge(nmlo_ok, b + 1)
                sp.dma_start(Qst[96:97, :, :], nm_hi[0:HEADS, :]).then_inc(nm_in, 16)
                sp.dma_start(Qst[97:98, :, :], nm_lo[0:HEADS, :]).then_inc(nm_in, 16)

            def load_xr(b):
                sp.wait_ge(st_out, 16 * 2 * NT * b)
                sp.dma_start(xr, dram_rows(x_rows, b * T, T).rearrange("(t p) d -> p t d", p=P)).then_inc(xr_in, 16)

            def store_rows(b):
                for t in range(NT):
                    sp.wait_ge(x3_ok, NT * b + t + 1)
                    sp.dma_start(dram_rows(x3d, b * T + t * P), x2[:, t, :]).then_inc(st_out, 16)
                for t in range(NT):
                    sp.wait_ge(h3_ok, NT * b + t + 1)
                    sp.dma_start(dram_rows(h3d, b * T + t * P), xr[:, t, :]).then_inc(st_out, 16)

            load_x(0)
            for lo, n, src in ((0, D, wq), (D, P, wk), (D + P, P, wv)):
                sp.dma_start(wstage[:, :, lo:lo + n], src.rearrange("(k p) n -> p k n", p=P)).then_inc(wqkv_in, 16)
            for dst, src in ((bqk_sb[:, 0:5], bqk), (cos_sb, cosT), (sin_sb, sinT), (bv_sb, bv), (wj_sb, wj),
                             (wi_sb[:, 0:1], wi), (bx_sb[:, 0:1], b_x), (bo_sb, bo)):
                sp.dma_start(dst, src).then_inc(par_in, 16)
            sp.dma_start(wo_sb, wo.rearrange("(k p) n -> p k n", p=P)).then_inc(par_in, 16)
            load_ctx(0)
            load_x(1)
            load_stacks(0)
            sp.wait_ge(zero_ok, 1)
            with sp.Fori(0, RT) as i:
                sp.dma_start(disp[bass.ds(i * P, P), :], zero).then_inc(zeroed, 16)

            def batch(b):
                load_negmax(b)
                if has(b, 2):
                    load_x(b + 2)
                if has(b, -1):
                    store_rows(b - 1)
                load_xr(b)
                if has(b, 1):
                    load_stacks(b + 1)
                    load_ctx(b + 1)

            batches(sp, batch)
            store_rows(B - 1)
            sp.wait_ge(zeroed, 16 * RT)
            sp.wait_ge(st_out, 16 * 2 * NT * B)

            sp.dma_start(g_f, gate.rearrange("(k p) e -> p k e", p=P)).then_inc(g_in, 16)

            for b in range(B):
                sp.dma_start(rows16[:, b * NT:(b + 1) * NT, :],
                             h3d[b * T:(b + 1) * T, :].rearrange("(t p) d -> p t d", p=P)).then_inc(row_in[b], 16)

            def tiles(base, n, mode):
                fb = base - TT
                first = 0 if mode == "shared" else ST
                src, src0 = (disp, 0) if mode == "routed" else (h3d, first * P)
                dst, dst0 = {"shared": (xsd, 0), "routed": (yd, 0), "final": (out_rows, first * P)}[mode]

                def load(i, slot):
                    if not (static(i) and i + fb < 2):
                        sp.wait_ge(bt_ps, i + (base - 1))
                    sp.dma_start(bx[:, slot, :], dram_rows(src, i * P + src0)).then_inc(b_in[slot], 16)

                def step(i, k, h):
                    if not static(i) or i + 2 < n:
                        load(i + 2, k)
                    if not static(i) or i >= 2:
                        sp.wait_ge(y_ok, i + (fb - 1))
                        sp.dma_start(dram_rows(dst, i * P + (dst0 - 2 * P)), yb[:, k, :]).then_inc(y_out[k], 16)
                        if mode == "final":
                            sp.wait_ge(fin_ok, i - 1)
                            sp.dma_start(out_rows[(i - 2) * P:(i - 1) * P, :], fin[:, i % 2, :])\
                                .then_inc(fin_out[i % 2], 16)
                    if mode != "routed" and i < n:
                        sp.dma_start(x3b[:, i % 2, :], x3d[(first + i) * P:(first + i + 1) * P, :])\
                            .then_inc(x3_in[i % 2], 16)
                    if mode == "final" and i < n:
                        sp.dma_start(xs[:, i % 2, :], xsd[i * P:(i + 1) * P, :]).then_inc(xs_in[i % 2], 16)
                    if mode == "shared" and i < n:
                        load_half(4 + i)
                    if mode == "shared" and 3 <= i < 3 + (TT + 2) // 3:
                        for t in range(3 * (i - 3), min(3 * (i - 2), TT)):
                            if t >= 2:
                                sp.wait_ge(sc_out[t % 2], 32 * (t // 2))
                            sp.dma_start(sx[:, t % 2, :], h3d[t * P:(t + 1) * P, :]).then_inc(sx_in[t % 2], 16)

                def load_half(u):
                    if u < 2 * (NE + 1 - SLAB) - 2:
                        sp.wait_ge(wlo_ok, 2 * SLAB + u + 1)
                        s, half = SLAB + 1 + u // 2, u % 2
                        o, _, cols, r = halves[half]
                        sp.dma_start(stage[:, o:o + cols].rearrange("p (k n) -> p k n", n=r),
                                     (w1, w2)[half][s].rearrange("(k p) n -> p k n", p=P)).then_inc(stage_sp[half], 16)

                for i in range(2):
                    load(i, (i + base) % 2)
                if mode == "shared":
                    for u in range(4):
                        load_half(u)
                pipeline(sp, base, n, step)

            tiles(TT, ST, "shared")
            for k in range(2):
                sp.wait_ge(sc_out[k], 32 * (TT // 2))
            tiles(TT + ST, RT, "routed")
            for k in range(2):
                sp.wait_ge(y_out[k], 16 * (ST // 2))
            tiles(TT + ST + RT, ST, "final")
            for k in range(2):
                sp.wait_ge(y_out[k], 16 * ((TT + RT + 1 - k) // 2))
                sp.wait_ge(fin_out[k], 16 * (ST // 2))

        @block.gpsimd
        def _(pool):
            pool.memset(ident[:, :], 0.0).then_inc(pz, 1)
            pool.memset(mk, 0.0).then_inc(pz, 1)
            pool.memset(ones32, 1.0).then_inc(consts_ok, 1)
            pool.memset(zero, 0.0).then_inc(zero_ok, 1)
            pool.wait_ge(pz, 2)
            pool.affine_select(out=ident[:, :], in_=ident[:, :], compare_op=ALU.not_equal, fill=1.0, base=0,
                               pattern=[[-1, P]], channel_multiplier=1).then_inc(consts_ok, 1)
            pool.affine_select(out=mk, in_=mk, compare_op=ALU.is_ge, fill=-1e30, base=0,
                               pattern=[[-1, P]], channel_multiplier=1).then_inc(consts_ok, 1)
            pool.wait_ge(consts_ok, 3)
            pool.tensor_copy(identb, ident[:, :]).then_inc(consts_ok, 1)

            def rope_cos(b):
                for k in range(5):
                    pool.wait_ge(qb_ok, 5 * b + k + 1)
                    pool.wait_ge(rope_ok, 5 * b + max(0, k - 1))
                    pool.tensor_tensor(t1[:, k % 2, :], qb[:, k % 2, :], cos_sb, ALU.mult).then_inc(t1_ok, 1)

            def add_bias(b):
                pool.wait_ge(xr_in, 16 * b + 16)
                for t in range(NT):
                    pool.tensor_tensor(xr[:, t, :], xr[:, t, :], bo_sb, ALU.add).then_inc(xrb_ok, 1)

            def select(b):
                for u in range(PAIRS):
                    wait_apart(pool, p_ok, PAIRS * b + u + 1, pool_waits)
                    blk = pT[:, u % 4, :, 0:P]
                    pool.affine_select(out=blk, in_=blk, compare_op=ALU.is_ge, fill=0.0, base=0,
                                       pattern=[[0, 2], [1, P]], channel_multiplier=-1).then_inc(mask_ok, 1)

            def load_expert(s):
                for h in range(2):
                    if not (static(s) and s == 0):
                        pool.wait_ge(wlo_ok, s * 2 + (h - 1))
                    src = (w1, w2)[h]
                    src = src[s:s + 1] if static(s) else src[bass.ds(s, 1)]
                    o, _, n, r = halves[h]
                    pool.dma_start(stage[:, o:o + n].rearrange("p (k n) -> p k n", n=r),
                                   src.rearrange("o (k p) n -> p (o k) n", p=P)).then_inc(stage_in[h], 16)

            pool.wait_ge(par_in, 16 * NPAR)
            rope_cos(0)
            pool.wait_ge(wqkv_ok, 1)
            load_expert(0)

            def batch(b):
                if has(b, 1):
                    rope_cos(b + 1)
                select(b)
                add_bias(b)
                if has(b, 1):
                    load_expert(b + 1)

            batches(pool, batch)

            pool.wait_ge(st_out, 16 * 2 * NT * B)
            pool.memset(lt_b, 1.0).then_inc(pz, 1)
            pool.memset(on_b, 1.0).then_inc(bconst, 1)
            pool.wait_ge(pz, 3)
            pool.affine_select(out=lt_b, in_=lt_b, compare_op=ALU.is_gt, fill=0.0, base=0,
                               pattern=[[1, P]], channel_multiplier=-1).then_inc(bconst, 1)
            for dst, pattern in ((iota8, [[0, TT], [1, NE]]), (it128, [[0, NE], [P, 16]]), (itile, [[1, RT], [0, NE]])):
                pool.iota(dst, pattern=pattern, base=0, channel_multiplier=0,
                          allow_small_or_imprecise_dtypes=True).then_inc(bconst, 1)
            pool.wait_ge(zeroed, 16 * RT)
            pool.wait_ge(route_ok, 1)
            for t in range(TT):
                pool.wait_ge(sx_in[t % 2], 16 * (t // 2) + 16)
                for c in range(2):
                    pool.indirect_dma_start(disp[:, :], bass.IndirectOffsetOnAxis(ap=slot_i[:, c, t:t + 1], axis=0),
                                            sx[:, t % 2, :], None).then_inc(sc_out[t % 2], 16)
            for k in range(2):
                pool.wait_ge(y_out[k], 16 * ((ST + RT + 1 - k) // 2))
            pool.wait_ge(dn_ps, ST + RT)
            for t in range(ST):
                if t >= 2:
                    pool.wait_ge(fin_ok, t - 1)
                    pool.wait_ge(y_ok, ST + RT + t - 1)
                for c in range(2):
                    pool.indirect_dma_start(gd[:, t % 2, c, :], None, yd[:, :],
                                            bass.IndirectOffsetOnAxis(ap=slot_i[:, c, ST + t:ST + t + 1], axis=0))\
                        .then_inc(gd_in[t % 2], 16)
                for c in range(2):
                    pool.indirect_dma_start(ge[:, t % 2, c, :], None, yd[:, :],
                                            bass.IndirectOffsetOnAxis(ap=slot_i[:, c, t:t + 1], axis=0))\
                        .then_inc(ge_in[t % 2], 16)

        @block.scalar
        def _(a):
            def project(b):
                a.wait_ge(proj_ok, 7 * b)
                for t in range(NT):
                    a.wait_ge(xt_ok, NT * b + t + 1)
                    a.activation(xhi[:, :, t * P:(t + 1) * P],
                                 ps[:, 6 + t % 2, :].rearrange("p (k t) -> p k t", k=KC), ACT.Copy).then_inc(xhi_ok, 1)
                for k in range(5):
                    a.wait_ge(proj_ok, 7 * b + k + 1)
                    a.wait_ge(rope_ok, 5 * b + max(0, k - 1))
                    a.activation(qb[:, k % 2, :], ps[:, PROJ_BANK[k], :], ACT.Identity,
                                 bias=bqk_sb[:, CHUNK[k]:CHUNK[k] + 1], scale=1.0 / WSCALE).then_inc(qb_ok, 1)

            def context(b):
                a.wait_ge(ctxT_ps, b + 1)
                a.activation(ctxT, ps[:, 4, :], ACT.Copy).then_inc(ctxT_ok, 1)
                a.wait_ge(sj_ps, b + 1)
                a.wait_ge(sib_ok, b + 1)
                a.wait_ge(x3_ok, NT * b)
                for t in range(NT):
                    a.activation(th[:, t, :], ps[:, 4, :], ACT.Tanh, bias=sib[:, t:t + 1], scale=0.5).then_inc(th_ok, 1)

            def negmax(b):
                a.wait_ge(mt_ps, b + 1)
                a.wait_ge(nm_in, 32 * b)
                a.activation(nm_hi[0:HEADS, :], ps[0:HEADS, 5, :], ACT.Copy, scale=-1.0).then_inc(nmhi_ok, 1)

            def exps(b):
                for u in range(PAIRS):
                    n = T - P * (u // 2 % NT)
                    a.wait_ge(pair_ok, PAIRS * (2 * b + 1) + u + 1) if static(b) else \
                        a.wait_ge(pair_ok, b * (2 * PAIRS) + (PAIRS + u + 1))
                    if not static(b) or PAIRS * b + u >= 4:
                        if static(b) or u >= 4:
                            a.wait_ge(pv_ok, PAIRS * b + (u - 3))
                        else:
                            a.wait_ge(pv_ok, PAIRS * b)
                    a.activation(pT[:, u % 4, :, 0:n], ps[:, 2 * (u % 2):2 * (u % 2) + 2, 0:n], ACT.Exp, scale=SC)\
                        .then_inc(p_ok, 1)

            def high_part(s, half):
                o, dst, n, _ = halves[half]
                if static(s) and s > SLAB:
                    a.wait_ge(stage_sp[half], (s - SLAB) * 16)
                else:
                    a.wait_ge(stage_in[half], s * 16 + 16)
                a.activation(w_cols(s * WN, dst, n), stage[:, o:o + n], ACT.Copy, scale=WSCALE).then_inc(whi_ok, 1)

            a.wait_ge(wqkv_in, 48)
            a.activation(wqkv_hi, wstage, ACT.Copy, scale=WSCALE).then_inc(wqkv_hi_ok, 1)
            a.wait_ge(par_in, 16 * NPAR)
            project(0)

            def copy_values(b):
                a.wait_ge(v_ok, 2 * b + 2)
                a.wait_ge(pv_ok, PAIRS * b)
                a.activation(V, Vn, ACT.Copy).then_inc(vc_ok, 1)

            copy_values(0)

            def batch(b):
                negmax(b)
                if has(b, 1):
                    project(b + 1)
                exps(b)
                context(b)
                if has(b, 1):
                    copy_values(b + 1)
                    for half in range(2):
                        high_part(b, half)

            batches(a, batch)

            def router():
                def step(i, k):
                    a.wait_ge(bt_ps, i + 1)
                    if not static(i) or i >= 2:
                        a.wait_ge(lg_ps, i - 1)
                    a.activation(bhi[:, k, :, :], ps[:, 6 * k, :].rearrange("p (k t) -> p k t", k=KC), ACT.Copy)\
                        .then_inc(bhi_ok, 1)

                step(0, 0)
                step(1, 1)
                for half in range(2):
                    high_part(SLAB, half)
                with a.Fori(1, TT // 2) as j:
                    step(j * 2, 0)
                    step(j * 2 + 1, 1)

            def tiles(base, n, mode):
                fb = base - TT

                def hi_part(i, k):
                    a.wait_ge(bt_ps, i + (base + 1))
                    if static(i) and i + fb < 2:
                        a.wait_ge(lg_ps, TT)
                    else:
                        a.wait_ge(up_ps, i + (fb - 1))
                    a.activation(bhi[:, k, :, :], ps[:, 0, :].rearrange("p (k t) -> p k t", k=KC), ACT.Copy)\
                        .then_inc(bhi_ok, 1)

                def step(i, k, h):
                    if not static(i) or i < n:
                        a.wait_ge(up_ps, i + (fb + 1))
                        if not static(i) or i + fb >= 2:
                            a.wait_ge(act_ok, i + (fb - 1))
                        a.activation(sil[:, k, :], ps[:, 1 + 2 * k, 0:FF], ACT.Silu, scale=1.0 / WSCALE)\
                            .then_inc(silu_ok, 1)
                    if not static(i) or i + 1 < n:
                        hi_part(i + 1, 1 - k)
                    if not static(i) or 1 <= i <= n:
                        a.wait_ge(at_ps, i + fb)
                        if not static(i) or i + fb >= 3:
                            a.wait_ge(dn_ps, i + (fb - 2))
                        a.activation(ahi[:, 1 - k, :, :], ps[:, 5, 0:3 * P].rearrange("p (k t) -> p k t", k=3), ACT.Copy)\
                            .then_inc(ahi_ok, 1)
                    if mode == "routed" and (not static(i) or i >= 2):
                        a.wait_ge(dn_ps, i + (fb - 1))
                        a.wait_ge(y_out[k], h * 16 + (fb // 2 - 1) * 16)
                        a.activation(yb[:, k, :], ps[:, 6, :], ACT.Copy, scale=1.0 / WSCALE).then_inc(y_ok, 1)
                    if mode == "shared" and i < n:
                        high_part(SLAB + 2 + i // 2, i % 2)
                        if i == 3:
                            a.wait_ge(diff_ok, 1)
                            a.activation(EX, EX, ACT.Exp).then_inc(e_ok, 1)

                hi_part(0, base % 2)
                if mode == "shared":
                    for half in range(2):
                        high_part(SLAB + 1, half)
                pipeline(a, base, n, step)

            a.wait_ge(h3_ok, NT * B)
            a.wait_ge(st_out, 16 * 2 * NT * B)
            router()
            tiles(TT, ST, "shared")
            tiles(TT + ST, RT, "routed")
            tiles(TT + ST + RT, ST, "final")

        @block.vector
        def _(v):
            def newton(ch, mv_, nw_):
                var, half, tmp, y = (nw_[:, i, :] for i in range(4))
                ch.link(v.tensor_scalar(var, mv_[:, :, 1], EPS, None, ALU.add))
                ch.link(v.tensor_scalar(tmp.bitcast(I32), var.bitcast(I32), 1, None, ALU.arith_shift_right))
                ch.link(v.tensor_scalar(half, var, -0.5, None, ALU.mult))
                ch.link(v.tensor_scalar(y.bitcast(I32), tmp.bitcast(I32), -1, MAGIC, ALU.mult, ALU.add))
                for _ in range(3):
                    ch.link(v.tensor_tensor(tmp, y, y, ALU.mult))
                    ch.link(v.tensor_tensor(tmp, tmp, half, ALU.mult))
                    ch.link(v.scalar_tensor_tensor(out=y, in0=tmp, scalar=1.5, in1=y, op0=ALU.add, op1=ALU.mult))

            def norm_stats(ch, src, st, mv_):
                for t in range(NT):
                    ins = v.bn_stats(st[:, t, :], src[:, t, :])
                ch.link(ins, v_waits)
                for t in range(NT):
                    ins = v.bn_aggr(mv_[:, t, :], st[:, t, :])
                ch.link(ins)

            def x_chain(b):
                return Chain(v, ch_ln, b * N_LN)

            def x_stats(b, ch):
                v.wait_ge(x_in, 16 * b + 16)
                norm_stats(ch, xb, stats, mv)

            def x_divide():
                for t in range(NT):
                    v.tensor_scalar(xb[:, t, :], xb[:, t, :], mv[:, t, 0:1], nw[:, 3, t:t + 1], ALU.subtract,
                                    ALU.mult).then_inc(xn_ok, 1)

            def norm_x(b):
                ch = x_chain(b)
                x_stats(b, ch)
                newton(ch, mv, nw)
                x_divide()

            def project(b):
                ch = Chain(v, ch_rope, b * N_ROPE)
                for t in range(NT):
                    v.wait_ge(xhi_ok, NT * b + t + 1)
                    v.tensor_tensor(xlo[:, :, t * P:(t + 1) * P],
                                    ps[:, 6 + t % 2, :].rearrange("p (k t) -> p k t", k=KC),
                                    xhi[:, :, t * P:(t + 1) * P], ALU.subtract).then_inc(xlo_ok, 1)
                wait_apart(v, vc_ok, b, v_waits)
                v.wait_ge(kst_in, 16 * 3 * KVH * b)
                v.wait_ge(qst_in, 16 * 3 * REP * b)
                for k, c in enumerate(CHUNK):
                    wait_apart(v, qb_ok, 5 * b + k + 1, v_waits)
                    ch.link(v.stream_shuffle(sh, qb[:, k % 2, :], [(i + DK // 2) % DK for i in range(DK)]))
                    ch.link(v.tensor_tensor(sh, sh, sin_sb, ALU.mult))
                    v.wait_ge(t1_ok, 5 * b + k + 1)
                    ch.link(v.tensor_tensor(rot, t1[:, k % 2, :], sh, ALU.add))
                    ch.link(v.tensor_copy(qk_hi[:, c, :], rot))
                    v.tensor_tensor(qk_lo[:, c, :], rot, qk_hi[:, c, :], ALU.subtract).then_inc(rope_ok, 1)
                    v.wait_ge(rope_ok, 5 * b + k + 1)
                assert ch.n == N_ROPE, ch.n

            def values(b):
                for half in range(2):
                    v.wait_ge(proj_ok, 7 * b + 6 + half)
                    for i in range(2):
                        ins = v.scalar_tensor_tensor(out=Vn[:, 2 * half + i, :],
                                                     in0=ps[:, V_BANK[half], i * P:(i + 1) * P], scalar=1.0 / WSCALE,
                                                     in1=bv_sb, op0=ALU.mult, op1=ALU.add)
                    ins.then_inc(v_ok, 1)

            def maxima(b):
                for u in range(PAIRS):
                    t, hp = u // (HEADS // 2), u % (HEADS // 2)
                    v.wait_ge(pair_ok, b * (2 * PAIRS) + (u + 1))
                    if u == 0:
                        v.wait_ge(mt_ps, b)
                    v.tensor_reduce(m[:, t, 2 * hp:2 * hp + 2], ps[:, 2 * (u % 2):2 * (u % 2) + 2, 0:P * (t + 1)],
                                    AX.X, ALU.max).then_inc(m_ok, 1)
                v.wait_ge(nmhi_ok, b + 1)
                v.scalar_tensor_tensor(out=nm_lo[0:HEADS, :], in0=ps[0:HEADS, 5, :], scalar=-1.0,
                                       in1=nm_hi[0:HEADS, :], op0=ALU.mult, op1=ALU.subtract).then_inc(nmlo_ok, 1)

            def normalise(b, c):
                v.wait_ge(pv_ok, PAIRS * b + (8 * c + 8))
                v.wait_ge(oT_ok, KVH * b + c)
                v.reciprocal(recip, ps[:, GROUP_BANK[c] + 1, :]).then_inc(rc_ok, 1)
                v.wait_ge(rc_ok, KVH * b + (c + 1))
                v.tensor_tensor(oT[:, c, :], ps[:, GROUP_BANK[c], :], recip, ALU.mult).then_inc(oT_ok, 1)

            def context(b):
                v.wait_ge(si_ps, b + 1)
                v.wait_ge(th_ok, NT * b)
                v.tensor_scalar(sib, ps[:, 5, 0:NT], bx_sb[:, 0:1], 0.5, ALU.add, ALU.mult).then_inc(sib_ok, 1)

            def add_output(b, t):
                if t == 0:
                    v.wait_ge(st_out, 16 * 2 * NT * b)
                v.wait_ge(op_ps, NT * b + (t + 1))
                v.wait_ge(xrb_ok, NT * b + (t + 1))
                v.tensor_tensor(x2[:, t, :], ps[:, OUT_BANK[t], :], xr[:, t, :], ALU.add).then_inc(x2_ok, 1)

            def after_chain(b):
                return Chain(v, ch_op, b * N_AFTER)

            def x2_stats(b, ch):
                v.wait_ge(x2_ok, NT * b + NT)
                norm_stats(ch, x2, stats2, mv2)
                newton(ch, mv2, nw2)
                ch.link(v.tensor_tensor(lnB, mv2[:, :, 0], nw2[:, 3, :], ALU.mult))
                v.tensor_scalar(lnA, nw2[:, 3, :], 0.4, 1.0, ALU.mult, ALU.add)
                ch.link(v.tensor_scalar(lnB, lnB, -0.4, 0.3, ALU.mult, ALU.add))

            def form_x3(b, ch):
                v.wait_ge(th_ok, NT * b + NT)
                for t in range(NT):
                    ch.link(v.tensor_scalar(x2[:, t, :], x2[:, t, :], lnA[:, t:t + 1], lnB[:, t:t + 1], ALU.mult,
                                            ALU.add))
                    v.scalar_tensor_tensor(out=x2[:, t, :], in0=th[:, t, :], scalar=0.3, in1=x2[:, t, :],
                                           op0=ALU.mult, op1=ALU.add).then_inc(x3_ok, 1)

            def x3_stats(b, ch):
                v.wait_ge(x3_ok, NT * b + NT)
                norm_stats(ch, x2, stats2, mv2)
                newton(ch, mv2, nw2)

            def form_h3(b, ch):
                for t in range(NT):
                    v.tensor_scalar(xr[:, t, :], x2[:, t, :], mv2[:, t, 0:1], nw2[:, 3, t:t + 1], ALU.subtract,
                                    ALU.mult).then_inc(h3_ok, 1)
                assert ch.n == N_AFTER, ch.n

            def low_part(s, half):
                o, dst, n, _ = halves[half]
                v.wait_ge(whi_ok, s * 2 + (half + 1))
                v.scalar_tensor_tensor(out=w_cols(s * WN, dst + n, n), in0=stage[:, o:o + n], scalar=WSCALE,
                                       in1=w_cols(s * WN, dst, n), op0=ALU.mult, op1=ALU.subtract).then_inc(wlo_ok, 1)

            v.memset(Kst[96:98, :, :], 1.0).then_inc(kones_ok, 1)
            v.wait_ge(wqkv_hi_ok, 1)
            v.scalar_tensor_tensor(out=wqkv_lo.rearrange("p k n -> p (k n)"), in0=stage[:, 0:KC * NQKV], scalar=WSCALE,
                                   in1=wqkv_hi.rearrange("p k n -> p (k n)"), op0=ALU.mult,
                                   op1=ALU.subtract).then_inc(wqkv_ok, 1)
            v.wait_ge(par_in, 16 * NPAR)
            norm_x(0)
            project(0)
            values(0)
            norm_x(1)

            def batch(b):
                maxima(b)
                if has(b, 1):
                    project(b + 1)
                    values(b + 1)
                ch = after_chain(b - 1) if has(b, -1) else None
                normalise(b, 0)
                if ch:
                    x2_stats(b - 1, ch)
                    form_x3(b - 1, ch)
                normalise(b, 1)
                if ch:
                    x3_stats(b - 1, ch)
                    form_h3(b - 1, ch)
                normalise(b, 2)
                normalise(b, 3)
                context(b)
                add_output(b, 0)
                if has(b, 2):
                    xch = x_chain(b + 2)
                    x_stats(b + 2, xch)
                if has(b, 1):
                    low_part(b, 0)
                add_output(b, 1)
                if has(b, 2):
                    newton(xch, mv, nw)
                if has(b, 1):
                    low_part(b, 1)
                add_output(b, 2)
                if has(b, 2):
                    x_divide()
                add_output(b, 3)

            batches(v, batch)
            ch = after_chain(B - 1)
            x2_stats(B - 1, ch)
            form_x3(B - 1, ch)
            x3_stats(B - 1, ch)
            form_h3(B - 1, ch)

            v.wait_ge(st_out, 16 * 2 * NT * B)
            rch = Chain(v, r_dve)
            v.wait_ge(g_in, 16)
            rch.link(v.tensor_scalar(g_f, g_f, WSCALE, None, ALU.mult))
            v.memset(ps[96:P, 5, 2 * P:3 * P], 0.0).then_inc(g_ok, 1)
            rch.link(v.tensor_copy(g_hi, g_f))
            v.tensor_tensor(g_lo, g_f, g_hi, ALU.subtract).then_inc(g_ok, 1)

            def router():
                def lo_part(i, k):
                    v.wait_ge(bhi_ok, i + 1)
                    v.tensor_tensor(blo[:, k, :, :], ps[:, 6 * k, :].rearrange("p (k t) -> p k t", k=KC), bhi[:, k, :, :],
                                    ALU.subtract).then_inc(blo_ok, 1)

                def take_logits(i, k):
                    v.wait_ge(lg_ps, i + 1)
                    row = LG[:, i, :] if static(i) else LG[:, bass.ds(i, 1), :].rearrange("p o e -> p (o e)")
                    v.tensor_scalar(row, ps[:, 7 - 2 * k, 0:NE], 1.0 / WSCALE, None, ALU.mult).then_inc(lg_ok, 1)

                lo_part(0, 0)
                lo_part(1, 1)
                take_logits(0, 0)
                for half in range(2):
                    low_part(SLAB, half)
                with v.Fori(1, TT // 2) as j:
                    lo_part(j * 2, 0)
                    take_logits(j * 2 - 1, 1)
                    lo_part(j * 2 + 1, 1)
                    take_logits(j * 2, 0)
                take_logits(TT - 1, 1)

            def best_two():
                v.wait_ge(bconst, 5)
                v.wait_ge(lg_ok, TT)
                for t in range(TT):
                    ins = v.max(srt[:, t, :], LG[:, t, :])
                rch.link(ins)
                for t in range(TT):
                    ins = v.max_index(sidx[:, t, :], srt[:, t, :], LG[:, t, :])
                rch.link(ins)
                v.tensor_tensor(EX, srt, srt[:, :, 0:1].to_broadcast([P, TT, NE]), ALU.subtract).then_inc(diff_ok, 1)
                for c in range(2):
                    rch.link(v.tensor_copy(idx_f[:, c, :], sidx[:, :, c]))
                for c, one_hot in ((0, M1), (1, M2)):
                    rch.link(v.tensor_tensor(one_hot, iota8, idx_f[:, c, :].unsqueeze(2).to_broadcast([P, TT, NE]),
                                             ALU.is_equal))
                v.tensor_tensor(Mb, M1.rearrange("p t e -> p (t e)"), M2.rearrange("p t e -> p (t e)"), ALU.add)\
                    .then_inc(mb_ok, 1)

            def count_pairs():
                v.wait_ge(cnt_ps, 1)
                tot = ps[:, 7, TT * NE:2 * TT * NE].rearrange("p (t e) -> p t e", t=TT)
                rch.link(v.memset(pre[:, 0, :], 0.0))
                for t in range(1, TT):
                    rch.link(v.tensor_tensor(pre[:, t, :], tot[:, t - 1, :], pre[:, t - 1, :], ALU.add))
                rch.link(v.tensor_tensor(nte[:, 0, :], tot[:, TT - 1, :], pre[:, TT - 1, :], ALU.add))
                rch.link(v.tensor_tensor(cmp, it128, nte[:, 0, :].unsqueeze(2).to_broadcast([P, NE, 16]), ALU.is_lt))
                rch.link(v.tensor_reduce(nte[:, 1, :], cmp, AX.X, ALU.add))
                rch.link(v.tensor_copy(nte[:, 2, 0:1], nte[:, 1, 0:1]))
                for e in range(1, NE):
                    rch.link(v.tensor_tensor(nte[:, 2, e:e + 1], nte[:, 2, e - 1:e], nte[:, 1, e:e + 1], ALU.add))

            def place_pairs():
                rch.link(v.tensor_tensor(cmt, itile, nte[:, 2:3, :].to_broadcast([P, RT, NE]), ALU.is_ge))
                rch.link(v.tensor_reduce(toff_f[:, 0:RT], cmt, AX.X, ALU.add))
                rch.link(v.tensor_scalar(toff_f[:, 0:RT], toff_f[:, 0:RT], float(NE - 1), float(WN), ALU.min, ALU.mult))
                v.tensor_scalar(toff[:, 0:RT], toff_f[:, 0:RT], float(WN), None, ALU.add).then_inc(table_ok, 1)
                rch.link(v.tensor_tensor(nte[:, 3, :], nte[:, 2, :], nte[:, 1, :], ALU.subtract))
                rch.link(v.tensor_scalar(nte[:, 3, :], nte[:, 3, :], float(P), None, ALU.mult))
                rch.link(v.tensor_tensor(R, ps[:, 7, 0:TT * NE].rearrange("p (t e) -> p t e", t=TT), pre, ALU.add))
                rch.link(v.tensor_tensor(R, R, nte[:, 3:4, :].to_broadcast([P, TT, NE]), ALU.add))
                for c, one_hot in ((0, M1), (1, M2)):
                    rch.link(v.tensor_tensor(one_hot, one_hot, R, ALU.mult))
                    rch.link(v.tensor_reduce(slot_f[:, c, :], one_hot, AX.X, ALU.add))
                v.tensor_copy(slot_i, slot_f).then_inc(route_ok, 1)

            def weigh_pairs():
                v.wait_ge(e_ok, 1)
                rch.link(v.tensor_reduce(zs[:, 0, :], EX, AX.X, ALU.add))
                rch.link(v.reciprocal(zs[:, 1, :], zs[:, 0, :]))
                for c in range(2):
                    rch.link(v.tensor_tensor(zs[:, 2 + c, :], EX[:, :, c], zs[:, 1, :], ALU.mult))
                rch.link(v.scalar_tensor_tensor(out=zs[:, 0, :], in0=zs[:, 2, :], scalar=1e-20, in1=zs[:, 3, :],
                                                op0=ALU.add, op1=ALU.add))
                rch.link(v.reciprocal(zs[:, 1, :], zs[:, 0, :]))
                for c in range(2):
                    rch.link(v.tensor_tensor(w12[:, c, :], zs[:, 2 + c, :], zs[:, 1, :], ALU.mult))


            routing = (best_two, count_pairs, place_pairs, weigh_pairs)

            def tiles(base, n, mode):
                fb = base - TT

                def lo_part(i, k):
                    v.wait_ge(bhi_ok, i + (base + 1))
                    v.tensor_tensor(blo[:, k, :, :], ps[:, 0, :].rearrange("p (k t) -> p k t", k=KC), bhi[:, k, :, :],
                                    ALU.subtract).then_inc(blo_ok, 1)

                def add_rows(acc, rows, t, k):
                    nonlocal added
                    for c in range(2):
                        ins = v.scalar_tensor_tensor(out=acc, in0=rows[:, k, c, :], scalar=w12[:, c, t:t + 1], in1=acc,
                                                     op0=ALU.mult, op1=ALU.add)
                        if c == 0:
                            added += 1
                            ins.then_inc(fch, 1)
                            v.wait_ge(fch, added)
                    return ins

                added = 0

                def step(i, k, h):
                    if not static(i) or i < n:
                        v.wait_ge(silu_ok, i + (fb + 1))
                        if not static(i) or i + fb >= 2:
                            v.wait_ge(at_ps, i + (fb - 1))
                        v.scalar_tensor_tensor(out=act[:, k, :], in0=ps[:, 2 + 2 * k, 0:FF], scalar=1.0 / WSCALE,
                                               in1=sil[:, k, :], op0=ALU.mult, op1=ALU.mult).then_inc(act_ok, 1)
                    if not static(i) or i + 1 < n:
                        lo_part(i + 1, 1 - k)
                    if not static(i) or 1 <= i <= n:
                        v.wait_ge(ahi_ok, i + fb)
                        v.tensor_tensor(alo[:, 1 - k, :, :], ps[:, 5, 0:3 * P].rearrange("p (k t) -> p k t", k=3),
                                        ahi[:, 1 - k, :, :], ALU.subtract).then_inc(alo_ok, 1)
                    if mode == "final" and i >= 2:
                        s, seen = i % 2, i // 2
                        v.wait_ge(xs_in[s], 16 * seen)
                        v.wait_ge(ge_in[s], 32 * seen)
                        add_rows(xs[:, s, :], ge, i - 2, s).then_inc(fx_ok, 1)
                        v.wait_ge(fx_ok, i - 1)
                        if i >= 4:
                            v.wait_ge(fin_out[s], 16 * (seen - 1))
                        v.tensor_copy(fin[:, s, :], xs[:, s, :]).then_inc(fin_ok, 1)
                        v.wait_ge(x3_in[s], 16 * (ST // 2 + seen))
                        v.wait_ge(gd_in[s], 32 * seen)
                        add_rows(x3b[:, s, :], gd, ST + i - 2, s).then_inc(x3g_ok, 1)
                        v.wait_ge(x3g_ok, i - 1)
                    if mode != "routed" and i >= 2:
                        s, seen = i % 2, i // 2
                        v.wait_ge(dn_ps, i + (fb - 1))
                        v.wait_ge(x3_in[s], 16 * seen + (16 * (ST // 2) if mode == "final" else 0))
                        if i + fb >= 4:
                            v.wait_ge(y_out[k], 16 * ((i - 2 + fb) // 2))
                        v.scalar_tensor_tensor(out=yb[:, k, :], in0=ps[:, 6, :], scalar=1.0 / WSCALE, in1=x3b[:, s, :],
                                               op0=ALU.mult, op1=ALU.add).then_inc(y_ok, 1)
                    if mode == "shared" and i < n:
                        if i < len(routing):
                            routing[i]()
                        low_part(SLAB + 2 + i // 2, i % 2)

                lo_part(0, base % 2)
                if mode == "shared":
                    for half in range(2):
                        low_part(SLAB + 1, half)
                pipeline(v, base, n, step)

            router()
            tiles(TT, ST, "shared")
            tiles(TT + ST, RT, "routed")
            tiles(TT + ST + RT, ST, "final")

        @block.tensor
        def _(pe):
            def project(b):
                for t in range(NT):
                    pe.wait_ge(xn_ok, NT * b + (t + 1))
                    if t < 2:
                        pe.wait_ge(v_ok, 2 * b)
                        pe.wait_ge(x2_ok, NT * b - NT if has(b, -2) else 0)
                    else:
                        pe.wait_ge(xlo_ok, NT * b + (t - 1))
                    for k in range(KC):
                        ins = pe.transpose(ps[:, 6 + t % 2, k * P:(k + 1) * P], xb[:, t, k * P:(k + 1) * P], ident[:, :])
                    ins.then_inc(xt_ok, 1)
                pe.wait_ge(xlo_ok, NT * b + NT)
                terms = ((wqkv_hi, xhi), (wqkv_hi, xlo), (wqkv_lo, xhi))
                for k, c in enumerate(CHUNK):
                    if k >= 2:
                        pe.wait_ge(qb_ok, 5 * b + (k - 1))
                    n = 0
                    for wpart, xpart in terms:
                        for kc in range(KC):
                            ins = pe.matmul(ps[:, PROJ_BANK[k], :], wpart[:, kc, c * P:(c + 1) * P], xpart[:, kc, :],
                                            start=(n == 0), stop=(n == 3 * KC - 1))
                            n += 1
                    ins.then_inc(proj_ok, 1)
                for half in range(2):
                    pe.wait_ge(qb_ok, 5 * b + (4 + half))
                    for i in range(2):
                        t, n = 2 * half + i, 0
                        for wpart, xpart in terms:
                            for kc in range(KC):
                                ins = pe.matmul(ps[:, V_BANK[half], i * P:(i + 1) * P], xpart[:, kc, t * P:(t + 1) * P],
                                                wpart[:, kc, D + P:NQKV], start=(n == 0), stop=(n == 3 * KC - 1))
                                n += 1
                    ins.then_inc(proj_ok, 1)

            def context(b):
                pe.wait_ge(ctx_ld, 16 * b + 16)
                pe.wait_ge(oT_ok, KVH * b + 3)
                for t in range(NT):
                    ins = pe.transpose(ps[:, 4, t * P:(t + 1) * P], ctx_sb[:, t, :], ident[:, :])
                ins.then_inc(ctxT_ps, 1)
                pe.wait_ge(ctxT_ok, b + 1)
                for t in range(NT):
                    ins = pe.matmul(ps[:, 5, t:t + 1], ctxT[:, t * P:(t + 1) * P], wi_sb[:, 0:1], start=True, stop=True)
                ins.then_inc(si_ps, 1)
                pe.matmul(ps[:, 4, :], wj_sb, ctxT, start=True, stop=True).then_inc(sj_ps, 1)

            def row_scores(b):
                pe.wait_ge(kst_in, 16 * 3 * KVH * b + 16 * 3 * KVH)
                pe.wait_ge(qst_in, 16 * 3 * REP * b + 16 * 3 * REP)
                for u in range(PAIRS):
                    t, hp = u // (HEADS // 2), u % (HEADS // 2)
                    if u < 2:
                        pe.wait_ge(p_ok, PAIRS * b)
                    else:
                        pe.wait_ge(m_ok, PAIRS * b + (u - 1))
                    for i in range(2):
                        h = 2 * hp + i
                        o = ps[:, 2 * (u % 2) + i, 0:P * (t + 1)]
                        pe.matmul(o, Qst[0:96, h, t * P:(t + 1) * P], Kst[0:96, h // REP, 0:P * (t + 1)],
                                  start=True, stop=False)
                        ins = pe.matmul(ps[:, 2 * (u % 2) + i, P * t:P * (t + 1)], identb, mk, start=False, stop=True)
                    ins.then_inc(pair_ok, 1)
                pe.wait_ge(m_ok, PAIRS * b + PAIRS)
                pe.wait_ge(x2_ok, NT * b)
                for t in range(NT):
                    ins = pe.transpose(ps[0:HEADS, 5, t * P:(t + 1) * P], m[:, t, :], ident[:, :])
                ins.then_inc(mt_ps, 1)

            def attend(b):
                LAG = 2

                def products(u):
                    c, j, r2 = u // 8, u // 2 % NT, u % 2
                    n = T - P * j
                    pe.wait_ge(mask_ok, PAIRS * b + (u + 1))
                    if u % 8 == 0:
                        if c == 0:
                            pe.wait_ge(vc_ok, b + 1)
                            pe.wait_ge(th_ok, NT * b)
                            pe.wait_ge(nmlo_ok, b + 1)
                        elif c == 1:
                            if has(b, 1):
                                pe.wait_ge(v_ok, 2 * b + 4)
                        else:
                            pe.wait_ge(oT_ok, KVH * b + (c - 1))
                    for bank, left in ((GROUP_BANK[c], V[:, j, c * DK:(c + 1) * DK]), (GROUP_BANK[c] + 1, ones32)):
                        for i in range(2):
                            r = 2 * r2 + i
                            ins = pe.matmul(ps[r * DK:(r + 1) * DK, bank, P * j:T], left, pT[:, u % 4, i, 0:n],
                                            start=(j == 0), stop=(j == NT - 1), tile_position=(0, r * DK))
                    ins.then_inc(pv_ok, 1)

                pe.wait_ge(nm_in, 32 * b + 32)
                for u in range(PAIRS + LAG):
                    if u < PAIRS:
                        c, j, r2 = u // 8, u // 2 % NT, u % 2
                        if u < 2:
                            pe.wait_ge(m_ok, PAIRS * b + PAIRS)
                        else:
                            pe.wait_ge(p_ok, PAIRS * b + (u - 1))
                        for i in range(2):
                            ins = pe.matmul(ps[:, 2 * (u % 2) + i, 0:T - P * j], Kst[0:98, c, P * j:P * (j + 1)],
                                            Qst[0:98, REP * c + 2 * r2 + i, P * j:T], start=True, stop=True)
                        ins.then_inc(pair_ok, 1)
                    if u >= LAG:
                        products(u - LAG)

            def output(b):
                pe.wait_ge(oT_ok, KVH * b + KVH)
                pe.wait_ge(sib_ok, b + 1)
                for t in range(NT):
                    if t >= 2:
                        pe.wait_ge(x2_ok, NT * b + (t - 1))
                    for c in range(KC):
                        ins = pe.matmul(ps[:, OUT_BANK[t], :], oT[:, c, t * P:(t + 1) * P], wo_sb[:, c, :],
                                        start=(c == 0), stop=(c == KC - 1))
                    ins.then_inc(op_ps, 1)

            pe.wait_ge(consts_ok, 4)
            pe.wait_ge(kones_ok, 1)
            pe.wait_ge(wqkv_ok, 1)
            project(0)
            pe.wait_ge(par_in, 16 * NPAR)

            def batch(b):
                row_scores(b)
                if has(b, 1):
                    project(b + 1)
                attend(b)
                context(b)
                output(b)

            batches(pe, batch)

            def router():
                def transpose_rows(i, k):
                    pe.wait_ge(row_in[i // NT], 16)
                    if i >= 2:
                        pe.wait_ge(blo_ok, i - 1)
                    for c in range(KC):
                        ins = pe.transpose(ps[:, 6 * k, c * P:(c + 1) * P], rows16[:, i, c * P:(c + 1) * P], ident[:, :])
                    ins.then_inc(bt_ps, 1)

                def logits(i, k):
                    pe.wait_ge(blo_ok, i + 1)
                    if i >= 2:
                        pe.wait_ge(lg_ok, i - 1)
                    n = 0
                    for left, g in ((bhi, g_hi), (bhi, g_lo), (blo, g_hi)):
                        for c in range(KC):
                            ins = pe.matmul(ps[:, 7 - 2 * k, 0:NE], left[:, k, c, :], g[:, c, :], start=(n == 0),
                                            stop=(n == 3 * KC - 1))
                            n += 1
                    ins.then_inc(lg_ps, 1)

                for i in range(TT + 1):
                    if i < TT:
                        transpose_rows(i, i % 2)
                    if i >= 1:
                        logits(i - 1, (i - 1) % 2)

            def tiles(base, n, mode):
                fb = base - TT

                def transpose_rows(i, k, h):
                    pe.wait_ge(b_in[k], 16 * ((i + fb) // 2 + 1) if static(i) else h * 16 + (fb // 2 + 1) * 16)
                    pe.wait_ge(blo_ok, i + base)
                    for c in range(KC):
                        ins = pe.transpose(ps[:, 0, c * P:(c + 1) * P], bx[:, k, c * P:(c + 1) * P], ident[:, :])
                    ins.then_inc(bt_ps, 1)

                def expert_of(i):
                    if mode != "routed":
                        return 0
                    at = toff[0:1, i:i + 1] if static(i) else toff[0:1, bass.ds(i, 1)]
                    return pe.value_load(at, min_val=WN, max_val=NE * WN)

                def up(i, k):
                    off = expert_of(i)
                    pe.wait_ge(blo_ok, i + (base + 1))
                    if not static(i) or i + fb >= 2:
                        pe.wait_ge(act_ok, i + (fb - 1))
                    n = 0
                    for left, part in ((bhi, 0), (bhi, 1), (blo, 0)):
                        for c in range(KC):
                            for g in range(2):
                                ins = pe.matmul(ps[:, 1 + 2 * k + g, 0:FF], left[:, k, c, :],
                                                w_cols(off, part * W1N + c * 2 * FF + g * FF, FF),
                                                start=(n == 0), stop=(n == 3 * KC - 1))
                            n += 1
                    ins.then_inc(up_ps, 1)

                def down(i, k):
                    off = expert_of(i)
                    pe.wait_ge(alo_ok, i + (fb + 1))
                    pe.wait_ge(y_ok, i + fb) if not static(i) or i + fb >= 1 else None
                    n = 0
                    for left, part in ((ahi, 0), (ahi, 1), (alo, 0)):
                        for c, (_, r) in enumerate(FCH):
                            ins = pe.matmul(ps[:, 6, :], left[0:r, k, c, :],
                                            w_cols(off, 2 * W1N + part * W2N + c * D, D, r), start=(n == 0), stop=(n == 8))
                            n += 1
                    ins.then_inc(dn_ps, 1)

                def step(i, k, h):
                    if not static(i) or i < n:
                        up(i, k)
                    if not static(i) or i + 1 < n:
                        transpose_rows(i + 1, 1 - k, h + i % 2 if static(i) else h + k)
                    if not static(i) or 1 <= i <= n:
                        pe.wait_ge(act_ok, i + fb)
                        if not static(i) or i + fb >= 2:
                            pe.wait_ge(alo_ok, i + (fb - 1))
                        for c, (o, r) in enumerate(FCH):
                            ins = pe.transpose(ps[0:r, 5, c * P:(c + 1) * P], act[:, 1 - k, o:o + r], ident[:, :])
                        ins.then_inc(at_ps, 1)
                    if not static(i) or i >= 2:
                        down(i - 2, k)
                    if mode == "shared" and i == 1:
                        pe.wait_ge(mb_ok, 1)
                        pe.wait_ge(lg_ok, TT)
                        pe.matmul(ps[:, 7, 0:TT * NE], lt_b, Mb, start=True, stop=True)
                        pe.matmul(ps[:, 7, TT * NE:2 * TT * NE], on_b, Mb, start=True, stop=True).then_inc(cnt_ps, 1)

                transpose_rows(0, base % 2, 0)
                pipeline(pe, base, n, step)

            pe.wait_ge(g_ok, 2)
            router()
            pe.wait_ge(wlo_ok, 2)
            tiles(TT, ST, "shared")
            pe.wait_ge(wlo_ok, 2 * (NE + 1))
            pe.wait_ge(table_ok, 1)
            pe.wait_ge(route_ok, 1)
            tiles(TT + ST, RT, "routed")
            tiles(TT + ST + RT, ST, "final")


def rope_tables():
    import numpy as np
    half = DK // 2
    inv = (1.0 / 10000.0 ** (np.arange(half, dtype=np.float32) / np.float32(half))).astype(np.float32)
    ang = np.arange(T, dtype=np.float32)[None, :] * inv[:, None]
    cos, sin = np.cos(ang).astype(np.float32), np.sin(ang).astype(np.float32)
    return (np.ascontiguousarray(np.tile(np.concatenate([cos, cos]), (P // DK, 1))),
            np.ascontiguousarray(np.tile(np.concatenate([-sin, sin]), (P // DK, 1))))


def kernel(**inputs):
    import numpy as np
    import concourse.bacc as bacc
    from concourse import mybir as mb
    from concourse.bass_utils import run_bass_kernel_spmd

    nc = bacc.Bacc("TRN2", target_bir_lowering=False, num_devices=1)
    g = {k: np.asarray(v) for k, v in inputs.items()}
    cosT, sinT = rope_tables()
    W12 = g["L0_xattn_W"]
    w1 = np.concatenate([np.concatenate([g["L0_ffn_sw1"].T, g["L0_ffn_sw2"].T], axis=1)[None], g["L0_ffn_w1"]])
    w2 = np.concatenate([g["L0_ffn_sw3"].T[None], g["L0_ffn_w2"]])
    w2 = np.concatenate([w2, np.zeros((NE + 1, len(FCH) * P - FF, D), np.float32)], axis=1)
    ins = {
        "x": g["x"], "ctx": g["ctx_512"], "wq": g["L0_attn_wq_w"], "wk": g["L0_attn_wk_w"], "wv": g["L0_attn_wv_w"],
        "bqk": np.concatenate([g["L0_attn_wq_b"], g["L0_attn_wk_b"]]).reshape(5, P).T,
        "bv": np.broadcast_to(g["L0_attn_wv_b"], (P, P)),
        "wo": g["L0_attn_o_w"], "bo": np.broadcast_to(g["L0_attn_o_b"], (P, D)),
        "wi": W12[0, :CTX].reshape(CTX, 1), "wj": np.broadcast_to(W12[0, CTX:].reshape(CTX, 1), (CTX, P)),
        "b_x": np.broadcast_to(g["L0_xattn_b"], (P, 1)), "gate": g["L0_ffn_gate_w"].T,
        "w1": w1, "w2": w2, "cosT": cosT, "sinT": sinT,
    }
    arrays, aps = {}, {}
    for name, a in ins.items():
        a = np.ascontiguousarray(a)
        arrays["in_" + name] = a
        aps[name] = nc.dram_tensor("in_" + name, a.shape, mb.dt.float32, kind="ExternalInput").ap()
    aps["out"] = nc.dram_tensor("out_0", (B, T, D), mb.dt.float32, kind="ExternalOutput").ap()
    for name, n in (("h3d", TOK), ("xsd", TOK), ("x3d", TOK), ("disp", RT * P), ("yd", RT * P)):
        aps[name] = nc.dram_tensor(name, (n, D), mb.dt.float32).ap()
    decoder_kernel(nc, **aps)
    r = run_bass_kernel_spmd(nc, [arrays], core_ids=[0])
    return r.results[0]["out_0"]
```

```python
from contextlib import ExitStack

import concourse.bass as bass
from concourse import mybir

F32 = mybir.dt.float32
F16 = mybir.dt.float16
BF16 = mybir.dt.bfloat16
I32 = mybir.dt.int32
U32 = mybir.dt.uint32
ALU = mybir.AluOpType
ACT = mybir.ActivationFunctionType
AX = mybir.AxisListType

B, T, D = 4, 512, 512
P = 128
NT = T // P
KC = D // P
HEADS, KVH, DK = 16, 4, 32
REP = HEADS // KVH
CTX = 128
NE, FF = 8, 352
TOK = B * T
TT = TOK // P
RT = (2 * TOK + NE * (P - 1)) // P
ST = TT // 2
FCH = [(0, 128), (128, 128), (256, 96)]
W1N = KC * 2 * FF
W2N = len(FCH) * D
WN = 2 * (W1N + W2N)
WSCALE = 256.0
EPS = 1e-5
MAGIC = 0x5F3759DF
NEWTON = 13
N_LN = 2 + NEWTON
N_ROPE = 4 * 5
N_AFTER = 2 * N_LN + 2 + NT
SLAB = 3
ARENA = 9552
NPAR = 8
PAIRS = KVH * NT * 2
CHUNK = [4, 0, 1, 2, 3]
PROJ_BANK = [6, 7, 6, 7, 6]
V_BANK = [7, 6]
GROUP_BANK = [4, 6, 4, 6]
OUT_BANK = [5, 7, 5, 7]
ROW_BANK = [0, 2, 6]
XT_BANK = [6, 7, 0, 1]
NQKV = D + 2 * P


def wait_apart(eng, sem, value, carrier):
    eng.wait_ge(sem, value)
    if not isinstance(value, int):
        eng.sem_inc(carrier, 1)


class Chain:

    def __init__(self, eng, sem, base=0):
        self.eng, self.sem, self.base, self.n = eng, sem, base, 0

    def link(self, ins, carrier=None):
        self.n += 1
        ins.then_inc(self.sem, 1)
        if carrier is None:
            self.eng.wait_ge(self.sem, self.base + self.n)
        else:
            wait_apart(self.eng, self.sem, self.base + self.n, carrier)


def decoder_kernel(nc, x, ctx, wq, wk, wv, bqk, bv, wo, bo, wi, wj, b_x, gate, w1, w2, cosT, sinT,
                   out, h3d, xsd, x3d, disp, yd):
    x_rows = x.rearrange("b t d -> (b t) d")
    out_rows = out.rearrange("b t d -> (b t) d")
    ctx_rows = ctx.rearrange("b t d -> (b t) d")
    SC = float(DK) ** -0.5

    with ExitStack() as stack:
        def sb(name, shape, dt):
            return stack.enter_context(nc.sbuf_tensor(name, shape, dt))

        def sem(name):
            return stack.enter_context(nc.semaphore(name))

        W = sb("W", [P, (NE + 1) * WN], F16)
        ident = sb("ident", [P, P], F32)
        stage = sb("stage", [P, W1N + W2N], F32)

        arena = sb("arena", [P, ARENA], F32)
        used = {"w": SLAB * WN // 2, "a": 0}
        Wf = W[:, :].bitcast(F32)

        def take(where, n):
            o = used[where]
            used[where] = o + n
            assert used[where] <= ((NE + 1) * WN // 2 if where == "w" else ARENA), (where, used)
            return (Wf if where == "w" else arena)[:, o:o + n]

        def take16(where, n):
            return take(where, n // 2).bitcast(F16)

        wstage = stage[:, 0:KC * NQKV].rearrange("p (k n) -> p k n", k=KC)
        stats = take("w", NT * 6).rearrange("p (t s) -> p t s", t=NT)
        mv = take("w", NT * 2).rearrange("p (t s) -> p t s", t=NT)
        stats2 = take("w", NT * 6).rearrange("p (t s) -> p t s", t=NT)
        mv2 = take("w", NT * 2).rearrange("p (t s) -> p t s", t=NT)
        nw = take("w", 16).rearrange("p (k t) -> p k t", k=4)
        nw2 = take("w", 16).rearrange("p (k t) -> p k t", k=4)
        sib = take("w", 4)
        lnA = take("w", 4)
        lnB = take("w", 4)
        bx_sb = take("w", 2)
        xb = take("w", NT * D).rearrange("p (t d) -> p t d", t=NT)
        xparts = take("w", KC * T)
        xhi = xparts[:, 0:KC * T // 2].bitcast(F16).rearrange("p (k t) -> p k t", k=KC)
        xlo = xparts[:, KC * T // 2:].bitcast(F16).rearrange("p (k t) -> p k t", k=KC)
        oT_hi, oT_lo = xhi, xlo
        wqkv_hi = take16("w", KC * NQKV).rearrange("p (k n) -> p k n", k=KC)
        wqkv_lo = take16("w", KC * NQKV).rearrange("p (k n) -> p k n", k=KC)
        wo_hi = take16("w", KC * D).rearrange("p (k n) -> p k n", k=KC)
        wo_lo = take16("w", KC * D).rearrange("p (k n) -> p k n", k=KC)
        pT = take("w", 4 * 2 * T).rearrange("p (s h q) -> p s h q", s=4, h=2)
        cos_sb = take("w", T)
        sin_sb = take("w", T)
        th = take("w", NT * T).rearrange("p (t m) -> p t m", t=NT)
        wo_stage = th
        Qst = take16("w", HEADS * T).rearrange("p (h t) -> p h t", h=HEADS)
        qk_hi = take16("w", 5 * T).rearrange("p (c t) -> p c t", c=5)
        qk_lo = take16("w", 5 * T).rearrange("p (c t) -> p c t", c=5)
        ctx_sb = take("w", NT * CTX).rearrange("p (t d) -> p t d", t=NT)
        ctxT = take("w", T)
        bo_sb = take("w", D)
        bv_sb = take("w", P)
        wj_sb = take("w", P)
        V = take("w", NT * P).rearrange("p (t d) -> p t d", t=NT)
        ones32 = take("w", DK)
        mk = take("w", P // 2).bitcast(BF16)
        identb = take("w", P // 2).bitcast(BF16)
        m = take("w", NT * HEADS).rearrange("p (t h) -> p t h", t=NT)
        bqk_sb = take("w", 6)
        wi_sb = take("w", 2)
        x3s = take("a", NT * D).rearrange("p (t d) -> p t d", t=NT)
        xr = take("a", NT * D).rearrange("p (t d) -> p t d", t=NT)
        Kst = take16("a", KVH * T).rearrange("p (c t) -> p c t", c=KVH)
        qb = take("a", 2 * T).rearrange("p (s t) -> p s t", s=2)
        t1 = take("a", 2 * T).rearrange("p (s t) -> p s t", s=2)
        sh = take("a", T)
        rot = take("a", T)
        recip = rot
        Vn = sh.rearrange("p (t d) -> p t d", t=NT)
        zero = take("a", D)
        nm_hi = take16("a", T)
        nm_lo = take16("a", T)

        ps = stack.enter_context(nc.psum_tensor("ps", [P, 8, 512], F32))

        consts_ok = sem("consts_ok")
        zero_ok = sem("zero_ok")
        zeroed = sem("zeroed")
        par_in = sem("par_in")
        wqkv_in = sem("wqkv_in")
        wqkv_ok = sem("wqkv_ok")
        x_in = sem("x_in")
        ctx_ld = sem("ctx_ld")
        xr_in = sem("xr_in")
        stage_in = [sem("stage_in_w1"), sem("stage_in_w2")]
        stage_sp = [sem("stage_sp_w1"), sem("stage_sp_w2")]
        kst_in = sem("kst_in")
        qst_in = sem("qst_in")
        nm_in = sem("nm_in")
        st_out = sem("st_out")
        xn_ok = sem("xn_ok")
        xt_ok = sem("xt_ok")
        xhi_ok = sem("xhi_ok")
        xlo_ok = sem("xlo_ok")
        proj_ok = sem("proj_ok")
        qb_ok = sem("qb_ok")
        t1_ok = sem("t1_ok")
        rope_ok = sem("rope_ok")
        v_ok = sem("v_ok")
        ctxT_ps = sem("ctxT_ps")
        ctxT_ok = sem("ctxT_ok")
        si_ps = sem("si_ps")
        sib_ok = sem("sib_ok")
        sj_ps = sem("sj_ps")
        th_ok = sem("th_ok")
        pair_ok = sem("pair_ok")
        m_ok = sem("m_ok")
        mt_ps = sem("mt_ps")
        nmhi_ok = sem("nmhi_ok")
        nmlo_ok = sem("nmlo_ok")
        p_ok = sem("p_ok")
        mask_ok = sem("mask_ok")
        pv_ok = sem("pv_ok")
        oT_ok = sem("oT_ok")
        oTp_ok = sem("oTp_ok")
        wo_in = sem("wo_in")
        wo_hi_ok = sem("wo_hi_ok")
        wo_ok = sem("wo_ok")
        xrb_ok = sem("xrb_ok")
        op_ps = sem("op_ps")
        x2_ok = sem("x2_ok")
        x3_ok = sem("x3_ok")
        h3_ok = sem("h3_ok")
        whi_ok = sem("whi_ok")
        wst_ok = sem("wst_ok")
        wlo_ok = sem("wlo_ok")
        row_in = [sem(f"row_in{i}") for i in range(B)]
        wqkv_hi_ok = sem("wqkv_hi_ok")
        rc_ok = sem("rc_ok")
        ch_ln = sem("ch_ln")
        ch_rope = sem("ch_rope")
        vc_ok = sem("vc_ok")
        ch_op = sem("ch_op")
        b_in = [sem(f"b_in{i}") for i in range(2)]
        x3_in = [sem(f"x3_in{i}") for i in range(2)]
        y_out = [sem(f"y_out{i}") for i in range(2)]
        bt_ps = sem("bt_ps")
        bhi_ok = sem("bhi_ok")
        blo_ok = sem("blo_ok")
        up_ps = sem("up_ps")
        silu_ok = sem("silu_ok")
        act_ok = sem("act_ok")
        at_ps = sem("at_ps")
        ahi_ok = sem("ahi_ok")
        alo_ok = sem("alo_ok")
        dn_ps = sem("dn_ps")
        y_ok = sem("y_ok")
        lg_ps = sem("lg_ps")
        lg_ok = sem("lg_ok")
        g_in = sem("g_in")
        g_ok = sem("g_ok")
        bconst = sem("bconst")
        e_ok = sem("e_ok")
        r_dve = sem("r_dve")
        cnt_ps = sem("cnt_ps")
        route_ok = sem("route_ok")
        sc_out = [sem("sc_out0"), sem("sc_out1")]
        gd_in = [sem("gd_in0"), sem("gd_in1")]
        ge_in = [sem("ge_in0"), sem("ge_in1")]
        xs_in = [sem("xs_in0"), sem("xs_in1")]
        fin_ok = sem("fin_ok")
        fch = sem("fch")
        fx_ok = sem("fx_ok")
        x3g_ok = sem("x3g_ok")
        fin_out = [sem("fin_out0"), sem("fin_out1")]
        pz = sem("pz")
        diff_ok = sem("diff_ok")
        kones_ok = sem("kones_ok")
        v_waits = sem("v_waits")
        pool_waits = sem("pool_waits")
        mb_ok = sem("mb_ok")
        table_ok = sem("table_ok")

        ub = {"o": 0}

        def takeb(n):
            o = ub["o"]
            ub["o"] = o + n
            assert ub["o"] <= ARENA, ub["o"]
            return arena[:, o:o + n]

        bx = takeb(2 * D).rearrange("p (s d) -> p s d", s=2)
        yb = takeb(2 * D).rearrange("p (s d) -> p s d", s=2)
        x3b = takeb(2 * D).rearrange("p (s d) -> p s d", s=2)
        cmp = takeb(NE * 16).rearrange("p (e k) -> p e k", e=NE)
        pre = takeb(TT * NE).rearrange("p (t e) -> p t e", t=TT)
        M1 = takeb(TT * NE).rearrange("p (t e) -> p t e", t=TT)
        M2 = takeb(TT * NE).rearrange("p (t e) -> p t e", t=TT)
        idx_f = takeb(2 * TT).rearrange("p (c t) -> p c t", c=2)
        w12 = takeb(2 * TT).rearrange("p (c t) -> p c t", c=2)
        slot_f = takeb(2 * TT).rearrange("p (c t) -> p c t", c=2)
        slot_i = takeb(2 * TT).bitcast(I32).rearrange("p (c t) -> p c t", c=2)
        zs = takeb(4 * TT).rearrange("p (c t) -> p c t", c=4)
        Mb = takeb(TT * NE // 2).bitcast(BF16)
        srt = takeb(TT * 8).rearrange("p (t e) -> p t e", t=TT)
        assert ub["o"] <= 2 * NT * D
        ub["o"] = 2 * NT * D
        bhi = takeb(D).bitcast(F16).rearrange("p (s k t) -> p s k t", s=2, k=KC)
        blo = takeb(D).bitcast(F16).rearrange("p (s k t) -> p s k t", s=2, k=KC)
        lsr = takeb(3 * TT * NE)
        LG = lsr[:, 0:TT * NE].rearrange("p (t e) -> p t e", t=TT)
        sidx = lsr[:, TT * NE:2 * TT * NE].bitcast(U32).rearrange("p (t e) -> p t e", t=TT)
        R = lsr[:, 2 * TT * NE:].rearrange("p (t e) -> p t e", t=TT)
        cmt = lsr[:, 0:RT * NE].rearrange("p (i e) -> p i e", i=RT)
        EX = takeb(TT * NE).rearrange("p (t e) -> p t e", t=TT)
        g_f = EX[:, 0:KC, :]
        g_hi = takeb(KC * NE // 2).bitcast(F16).rearrange("p (k e) -> p k e", k=KC)
        g_lo = takeb(KC * NE // 2).bitcast(F16).rearrange("p (k e) -> p k e", k=KC)
        sil = takeb(2 * FF).rearrange("p (s f) -> p s f", s=2)
        act = takeb(2 * FF).rearrange("p (s f) -> p s f", s=2)
        ahi = takeb(3 * P).bitcast(F16).rearrange("p (s k t) -> p s k t", s=2, k=3)
        alo = takeb(3 * P).bitcast(F16).rearrange("p (s k t) -> p s k t", s=2, k=3)
        iota8 = takeb(TT * NE).rearrange("p (t e) -> p t e", t=TT)
        it128 = takeb(NE * 16).rearrange("p (e k) -> p e k", e=NE)
        itile = takeb(RT * NE).rearrange("p (i e) -> p i e", i=RT)
        lt_b = takeb(P // 2).bitcast(BF16)
        on_b = takeb(P // 2).bitcast(BF16)
        nte = takeb(4 * NE).rearrange("p (c e) -> p c e", c=4)
        toff_f = takeb(RT + 1)
        toff = takeb(RT + 1).bitcast(I32)
        rows16 = Wf[:, (NE - 1) * WN // 2:(NE - 1) * WN // 2 + TT * D].rearrange("p (t d) -> p t d", t=TT)
        fb0 = WN // 2
        gd = Wf[:, fb0:fb0 + 4 * D].rearrange("p (s c d) -> p s c d", s=2, c=2)
        ge = Wf[:, fb0 + 4 * D:fb0 + 8 * D].rearrange("p (s c d) -> p s c d", s=2, c=2)
        fin = stage[:, 4 * D:6 * D].rearrange("p (s d) -> p s d", s=2)
        xs = stage[:, 6 * D:8 * D].rearrange("p (s d) -> p s d", s=2)

        def static(v):
            return isinstance(v, int)

        def w_cols(off, o, n, rows_=P):
            return W[0:rows_, off + o:off + o + n] if static(off) else W[0:rows_, bass.ds(off + o, n)]

        def dram_rows(t_, base, n=P):
            return t_[base:base + n, :] if static(base) else t_[bass.ds(base, n), :]

        def pipeline(eng, base, n, step):
            loops = max(0, (n - 6) // 2) if n > ST else 0
            first = 4 if loops else 0
            for i in range(first):
                step(i, (i + base) % 2, i // 2)
            if loops:
                with eng.Fori(0, loops) as j:
                    step(j * 2 + 4, 0, j + 2)
                    step(j * 2 + 5, 1, j + 2)
            for i in range(first + 2 * loops, n + 2):
                step(i, (i + base) % 2, i // 2)

        def batches(eng, stage_fn):
            stage_fn(0)
            with eng.Fori(1, B - 2) as b:
                stage_fn(b)
            stage_fn(B - 2)
            stage_fn(B - 1)

        def has(b, ahead):
            return not static(b) or 0 <= b + ahead < B

        first_rows = -(-(WN // 2) // D)
        units_at = ((), (0, 1), (2,), (3, 4), (5,), (6, 7), (8,), (9,), (10,), (11,))

        halves = ((0, 0, W1N, 2 * FF), (W1N, 2 * W1N, W2N, D))

        def h3_place(b):
            return xr if static(b) and b == B - 1 else x3s

        block = stack.enter_context(nc.Block())

        @block.sync
        def _(sp):
            def load_x(b):
                sp.wait_ge(xt_ok, b * NT)
                sp.dma_start(xb, dram_rows(x_rows, b * T, T).rearrange("(t p) d -> p t d", p=P)).then_inc(x_in, 16)

            def load_ctx(b):
                sp.wait_ge(ctxT_ps, b)
                sp.dma_start(ctx_sb, dram_rows(ctx_rows, b * T, T).rearrange("(t p) d -> p t d", p=P))\
                    .then_inc(ctx_ld, 16)

            def load_stacks(b):
                sp.wait_ge(pair_ok, 2 * PAIRS * b)
                sp.wait_ge(rope_ok, 5 * b + 1)
                for c in range(KVH):
                    k_hi, k_lo = qk_hi[32 * c:32 * c + 32, 4, :], qk_lo[32 * c:32 * c + 32, 4, :]
                    for at, src in ((0, k_hi), (32, k_hi), (64, k_lo)):
                        sp.dma_start(Kst[at:at + 32, c, :], src).then_inc(kst_in, 16)
                sp.wait_ge(rope_ok, 5 * b + 5)
                for r in range(REP):
                    q_hi, q_lo = qk_hi[32 * r:32 * r + 32, 0:4, :], qk_lo[32 * r:32 * r + 32, 0:4, :]
                    for at, src in ((0, q_hi), (32, q_lo), (64, q_hi)):
                        sp.dma_start(Qst[at:at + 32, r:HEADS:REP, :], src).then_inc(qst_in, 16)

            def load_negmax(b):
                sp.wait_ge(nmhi_ok, b + 1)
                sp.wait_ge(nmlo_ok, b + 1)
                sp.dma_start(Qst[96:97, :, :], nm_hi[0:HEADS, :]).then_inc(nm_in, 16)
                sp.dma_start(Qst[97:98, :, :], nm_lo[0:HEADS, :]).then_inc(nm_in, 16)

            def load_xr(b):
                sp.wait_ge(x3_ok, NT * b)
                sp.dma_start(xr, dram_rows(x_rows, b * T, T).rearrange("(t p) d -> p t d", p=P)).then_inc(xr_in, 16)

            def store_x3(b):
                for t in range(NT):
                    sp.wait_ge(x3_ok, NT * b + t + 1)
                    sp.dma_start(dram_rows(x3d, b * T + t * P), x3s[:, t, :]).then_inc(st_out, 16)

            def store_h3(b):
                for t in range(NT):
                    sp.wait_ge(h3_ok, NT * b + t + 1)
                    sp.dma_start(dram_rows(h3d, b * T + t * P), h3_place(b)[:, t, :]).then_inc(st_out, 16)

            load_x(0)
            for lo, n, src in ((0, D, wq), (D, P, wk), (D + P, P, wv)):
                sp.dma_start(wstage[:, :, lo:lo + n], src.rearrange("(k p) n -> p k n", p=P)).then_inc(wqkv_in, 16)
            for dst, src in ((bqk_sb[:, 0:5], bqk), (cos_sb, cosT), (sin_sb, sinT), (bv_sb, bv), (wj_sb, wj),
                             (wi_sb[:, 0:1], wi), (bx_sb[:, 0:1], b_x), (bo_sb, bo)):
                sp.dma_start(dst, src).then_inc(par_in, 16)
            sp.dma_start(wo_stage, wo.rearrange("(k p) n -> p k n", p=P)).then_inc(wo_in, 16)
            load_ctx(0)
            load_x(1)
            load_stacks(0)
            sp.wait_ge(zero_ok, 1)
            with sp.Fori(0, RT) as i:
                sp.dma_start(disp[bass.ds(i * P, P), :], zero).then_inc(zeroed, 16)

            def batch(b):
                load_negmax(b)
                if has(b, 2):
                    load_x(b + 2)
                if has(b, -1):
                    store_x3(b - 1)
                load_xr(b)
                if has(b, 1):
                    load_stacks(b + 1)
                    load_ctx(b + 1)
                if has(b, -1):
                    store_h3(b - 1)

            batches(sp, batch)
            sp.wait_ge(sj_ps, B)
            sp.wait_ge(xrb_ok, NT * B)
            sp.dma_start(g_f, gate.rearrange("(k p) e -> p k e", p=P)).then_inc(g_in, 16)

            def load_rows(b):
                sp.dma_start(rows16[:, b * NT:(b + 1) * NT, :],
                             h3d[b * T:(b + 1) * T, :].rearrange("(t p) d -> p t d", p=P)).then_inc(row_in[b], 16)

            sp.wait_ge(st_out, 16 * 2 * NT * (B - 1))
            for b in range(B - 1):
                load_rows(b)
            store_x3(B - 1)
            store_h3(B - 1)
            sp.wait_ge(zeroed, 16 * RT)
            sp.wait_ge(st_out, 16 * 2 * NT * B)

            def tiles(base, n, mode):
                fb = base - TT
                first = 0 if mode == "shared" else ST
                src, src0 = (disp, 0) if mode == "routed" else (h3d, first * P)
                dst, dst0 = {"shared": (xsd, 0), "routed": (yd, 0), "final": (out_rows, first * P)}[mode]

                def load(i, slot, src=src, src0=src0):
                    if not (static(i) and i + fb < 2):
                        sp.wait_ge(bt_ps, i + (base - 1))
                    sp.dma_start(bx[:, slot, :], dram_rows(src, i * P + src0)).then_inc(b_in[slot], 16)

                def step(i, k, h):
                    if not static(i) or i + 2 < n:
                        load(i + 2, k)
                    elif mode == "routed" and i < n:
                        load(i + 2, k, h3d, (ST - n) * P)
                    if not static(i) or i >= 2:
                        sp.wait_ge(y_ok, i + (fb - 1))
                        sp.dma_start(dram_rows(dst, i * P + (dst0 - 2 * P)), yb[:, k, :]).then_inc(y_out[k], 16)
                        if mode == "final":
                            sp.wait_ge(fin_ok, i - 1)
                            sp.dma_start(out_rows[(i - 2) * P:(i - 1) * P, :], fin[:, i % 2, :])\
                                .then_inc(fin_out[i % 2], 16)
                    if mode != "routed" and i < n:
                        sp.dma_start(x3b[:, i % 2, :], x3d[(first + i) * P:(first + i + 1) * P, :])\
                            .then_inc(x3_in[i % 2], 16)
                    if mode == "final" and i < n:
                        sp.dma_start(xs[:, i % 2, :], xsd[i * P:(i + 1) * P, :]).then_inc(xs_in[i % 2], 16)
                    if mode == "shared":
                        for u in units_at[i]:
                            load_half(2 + u)

                def load_half(u):
                    if u < 2 * (NE + 1 - SLAB):
                        sp.wait_ge(wlo_ok, 2 * SLAB + u - 1)
                        s, half = SLAB + u // 2, u % 2
                        o, _, cols, r = halves[half]
                        sp.dma_start(stage[:, o:o + cols].rearrange("p (k n) -> p k n", n=r),
                                     (w1, w2)[half][s].rearrange("(k p) n -> p k n", p=P)).then_inc(stage_sp[half], 16)

                if mode != "final":
                    for i in range(2):
                        load(i, (i + base) % 2)
                if mode == "shared":
                    load_rows(B - 1)
                pipeline(sp, base, n, step)

            tiles(TT, ST, "shared")
            sp.wait_ge(sc_out[0], 32 * first_rows)
            sp.wait_ge(sc_out[1], 32 * (TT - first_rows))
            tiles(TT + ST, RT, "routed")
            for k in range(2):
                sp.wait_ge(y_out[k], 16 * (ST // 2))
            tiles(TT + ST + RT, ST, "final")
            for k in range(2):
                sp.wait_ge(y_out[k], 16 * ((TT + RT + 1 - k) // 2))
                sp.wait_ge(fin_out[k], 16 * (ST // 2))

        @block.gpsimd
        def _(pool):
            pool.memset(ident[:, :], 0.0).then_inc(pz, 1)
            pool.memset(mk, 0.0).then_inc(pz, 1)
            pool.memset(ones32, 1.0).then_inc(consts_ok, 1)
            pool.memset(zero, 0.0).then_inc(zero_ok, 1)
            pool.wait_ge(pz, 2)
            pool.affine_select(out=ident[:, :], in_=ident[:, :], compare_op=ALU.not_equal, fill=1.0, base=0,
                               pattern=[[-1, P]], channel_multiplier=1).then_inc(consts_ok, 1)
            pool.affine_select(out=mk, in_=mk, compare_op=ALU.is_ge, fill=-1e30, base=0,
                               pattern=[[-1, P]], channel_multiplier=1).then_inc(consts_ok, 1)
            pool.wait_ge(consts_ok, 3)
            pool.tensor_copy(identb, ident[:, :]).then_inc(consts_ok, 1)

            def rope_cos(b):
                for k in range(5):
                    pool.wait_ge(qb_ok, 5 * b + k + 1)
                    pool.wait_ge(rope_ok, 5 * b + max(0, k - 1))
                    pool.tensor_tensor(t1[:, k % 2, :], qb[:, k % 2, :], cos_sb, ALU.mult).then_inc(t1_ok, 1)

            def add_bias(b):
                pool.wait_ge(xr_in, 16 * b + 16)
                for t in range(NT):
                    pool.tensor_tensor(xr[:, t, :], xr[:, t, :], bo_sb, ALU.add).then_inc(xrb_ok, 1)

            def select(b):
                for u in range(PAIRS):
                    wait_apart(pool, p_ok, PAIRS * b + u + 1, pool_waits)
                    blk = pT[:, u % 4, :, 0:P]
                    pool.affine_select(out=blk, in_=blk, compare_op=ALU.is_ge, fill=0.0, base=0,
                                       pattern=[[0, 2], [1, P]], channel_multiplier=-1).then_inc(mask_ok, 1)

            def load_half(s, h):
                src = (w1, w2)[h]
                src = src[s:s + 1] if static(s) else src[bass.ds(s, 1)]
                o, _, n, r = halves[h]
                pool.dma_start(stage[:, o:o + n].rearrange("p (k n) -> p k n", n=r),
                               src.rearrange("o (k p) n -> p (o k) n", p=P)).then_inc(stage_in[h], 16)

            def low_parts(s):
                for h, (o, dst, n, _) in enumerate(halves):
                    pool.wait_ge(wst_ok, s * 2 + (h + 1))
                    pool.tensor_tensor(w_cols(s * WN, dst + n, n), stage[:, o:o + n], w_cols(s * WN, dst, n),
                                       ALU.subtract).then_inc(wlo_ok, 1)
                    pool.wait_ge(wlo_ok, s * 2 + (h + 1))
                    load_half(s + 1, h)

            pool.wait_ge(par_in, 16 * NPAR)
            rope_cos(0)
            pool.wait_ge(wqkv_ok, 1)
            pool.wait_ge(qst_in, 16 * 3 * REP)
            for h in range(2):
                load_half(0, h)

            def batch(b):
                if has(b, 1):
                    rope_cos(b + 1)
                select(b)
                add_bias(b)
                if has(b, 1):
                    low_parts(b)

            batches(pool, batch)

            pool.wait_ge(st_out, 16 * 2 * NT * B)
            pool.memset(lt_b, 1.0).then_inc(pz, 1)
            pool.memset(on_b, 1.0).then_inc(bconst, 1)
            pool.wait_ge(pz, 3)
            pool.affine_select(out=lt_b, in_=lt_b, compare_op=ALU.is_gt, fill=0.0, base=0,
                               pattern=[[1, P]], channel_multiplier=-1).then_inc(bconst, 1)
            for dst, pattern in ((iota8, [[0, TT], [1, NE]]), (it128, [[0, NE], [P, 16]]), (itile, [[1, RT], [0, NE]])):
                pool.iota(dst, pattern=pattern, base=0, channel_multiplier=0,
                          allow_small_or_imprecise_dtypes=True).then_inc(bconst, 1)
            pool.wait_ge(zeroed, 16 * RT)
            pool.wait_ge(route_ok, 1)
            for t in range(TT):
                if t % NT == 0:
                    pool.wait_ge(row_in[t // NT], 16)
                for c in range(2):
                    pool.indirect_dma_start(disp[:, :], bass.IndirectOffsetOnAxis(ap=slot_i[:, c, t:t + 1], axis=0),
                                            rows16[:, t, :], None).then_inc(sc_out[int(t >= first_rows)], 16)
            for k in range(2):
                pool.wait_ge(y_out[k], 16 * ((ST + RT + 1 - k) // 2))
            pool.wait_ge(dn_ps, ST + RT)
            for t in range(ST):
                if t >= 2:
                    pool.wait_ge(fin_ok, t - 1)
                    pool.wait_ge(y_ok, ST + RT + t - 1)
                for c in range(2):
                    pool.indirect_dma_start(gd[:, t % 2, c, :], None, yd[:, :],
                                            bass.IndirectOffsetOnAxis(ap=slot_i[:, c, ST + t:ST + t + 1], axis=0))\
                        .then_inc(gd_in[t % 2], 16)
                for c in range(2):
                    pool.indirect_dma_start(ge[:, t % 2, c, :], None, yd[:, :],
                                            bass.IndirectOffsetOnAxis(ap=slot_i[:, c, t:t + 1], axis=0))\
                        .then_inc(ge_in[t % 2], 16)

        @block.scalar
        def _(a):
            def project(b):
                a.wait_ge(proj_ok, 7 * b)
                for t in range(NT):
                    a.wait_ge(xt_ok, NT * b + t + 1)
                    a.activation(xhi[:, :, t * P:(t + 1) * P],
                                 ps[:, XT_BANK[t], :].rearrange("p (k t) -> p k t", k=KC), ACT.Copy).then_inc(xhi_ok, 1)
                if static(b) and b == 0:
                    a.wait_ge(par_in, 16 * NPAR)
                for k in range(5):
                    a.wait_ge(proj_ok, 7 * b + k + 1)
                    a.wait_ge(rope_ok, 5 * b + max(0, k - 1))
                    a.activation(qb[:, k % 2, :], ps[:, PROJ_BANK[k], :], ACT.Identity,
                                 bias=bqk_sb[:, CHUNK[k]:CHUNK[k] + 1], scale=1.0 / WSCALE).then_inc(qb_ok, 1)

            def context(b):
                a.wait_ge(ctxT_ps, b + 1)
                a.activation(ctxT, ps[:, 4, :], ACT.Copy).then_inc(ctxT_ok, 1)
                a.wait_ge(sj_ps, b + 1)
                a.wait_ge(sib_ok, b + 1)
                a.wait_ge(x3_ok, NT * b)
                if static(b) and b == 0:
                    a.wait_ge(wo_ok, 1)
                for t in range(NT):
                    a.activation(th[:, t, :], ps[:, 4, :], ACT.Tanh, bias=sib[:, t:t + 1], scale=0.5).then_inc(th_ok, 1)

            def negmax(b):
                a.wait_ge(mt_ps, b + 1)
                a.wait_ge(nm_in, 32 * b)
                a.activation(nm_hi[0:HEADS, :], ps[0:HEADS, 5, :], ACT.Copy, scale=-1.0).then_inc(nmhi_ok, 1)

            def exps(b):
                for u in range(PAIRS):
                    n = T - P * (u // 2 % NT)
                    a.wait_ge(pair_ok, PAIRS * (2 * b + 1) + u + 1) if static(b) else \
                        a.wait_ge(pair_ok, b * (2 * PAIRS) + (PAIRS + u + 1))
                    if not static(b) or PAIRS * b + u >= 4:
                        if static(b) or u >= 4:
                            a.wait_ge(pv_ok, PAIRS * b + (u - 3))
                        else:
                            a.wait_ge(pv_ok, PAIRS * b)
                    a.activation(pT[:, u % 4, :, 0:n], ps[:, 2 * (u % 2):2 * (u % 2) + 2, 0:n], ACT.Exp, scale=SC)\
                        .then_inc(p_ok, 1)

            def high_part(s, half):
                o, dst, n, _ = halves[half]
                if static(s) and s > SLAB:
                    a.wait_ge(stage_sp[half], (s - SLAB) * 16)
                    if s >= NE - 1:
                        a.wait_ge(sc_out[0], 32 * first_rows)
                    if s == NE:
                        a.wait_ge(sc_out[1], 32 * (TT - first_rows))
                else:
                    a.wait_ge(stage_in[half], s * 16 + 16)
                a.activation(w_cols(s * WN, dst, n), stage[:, o:o + n], ACT.Copy, scale=WSCALE).then_inc(whi_ok, 1)

            def scale_stage(s, half):
                st = stage[:, halves[half][0]:halves[half][0] + halves[half][2]]
                a.wait_ge(whi_ok, s * 2 + (half + 1))
                a.activation(st, st, ACT.Copy, scale=WSCALE).then_inc(wst_ok, 1)

            a.wait_ge(wqkv_in, 48)
            a.activation(wqkv_hi[:, :, 0:D], wstage[:, :, 0:D], ACT.Copy, scale=WSCALE)
            a.activation(wqkv_hi[:, :, D:NQKV], wstage[:, :, D:NQKV], ACT.Copy, scale=WSCALE).then_inc(wqkv_hi_ok, 1)
            project(0)

            def copy_values(b):
                a.wait_ge(v_ok, 2 * b + 2)
                a.wait_ge(pv_ok, PAIRS * b)
                a.activation(V, Vn, ACT.Copy).then_inc(vc_ok, 1)

            copy_values(0)
            a.wait_ge(wo_in, 16)
            a.activation(wo_hi, wo_stage, ACT.Copy, scale=WSCALE).then_inc(wo_hi_ok, 1)

            def batch(b):
                negmax(b)
                if has(b, 1):
                    project(b + 1)
                exps(b)
                context(b)
                if has(b, 1):
                    copy_values(b + 1)
                    for half in range(2):
                        high_part(b, half)
                        scale_stage(b, half)

            batches(a, batch)

            def router():
                def step(i, k):
                    a.wait_ge(bt_ps, i + 1)
                    if not static(i) or i >= 2:
                        a.wait_ge(lg_ps, i - 1)
                    a.activation(bhi[:, k, :, :], ps[:, 6 * k, :].rearrange("p (k t) -> p k t", k=KC), ACT.Copy)\
                        .then_inc(bhi_ok, 1)

                step(0, 0)
                step(1, 1)
                with a.Fori(1, TT // 2) as j:
                    step(j * 2, 0)
                    step(j * 2 + 1, 1)

            def tiles(base, n, mode):
                fb = base - TT

                def hi_part(i, k):
                    a.wait_ge(bt_ps, i + (base + 1))
                    if static(i) and i + fb < 2:
                        a.wait_ge(lg_ps, TT)
                    else:
                        a.wait_ge(up_ps, i + (fb - 1))
                    a.activation(bhi[:, k, :, :], ps[:, 0, :].rearrange("p (k t) -> p k t", k=KC), ACT.Copy)\
                        .then_inc(bhi_ok, 1)

                def step(i, k, h):
                    if not static(i) or i < n:
                        a.wait_ge(up_ps, i + (fb + 1))
                        if not static(i) or i + fb >= 2:
                            a.wait_ge(act_ok, i + (fb - 1))
                        a.activation(sil[:, k, :], ps[:, 1 + 2 * k, 0:FF], ACT.Silu, scale=1.0 / WSCALE)\
                            .then_inc(silu_ok, 1)
                    if not static(i) or i + 1 < n:
                        hi_part(i + 1, 1 - k)
                    if not static(i) or 1 <= i <= n:
                        a.wait_ge(at_ps, i + fb)
                        if not static(i) or i + fb >= 3:
                            a.wait_ge(dn_ps, i + (fb - 2))
                        a.activation(ahi[:, 1 - k, :, :], ps[:, 5, 0:3 * P].rearrange("p (k t) -> p k t", k=3), ACT.Copy)\
                            .then_inc(ahi_ok, 1)
                    if mode == "routed" and (not static(i) or i >= 2):
                        a.wait_ge(dn_ps, i + (fb - 1))
                        a.wait_ge(y_out[k], h * 16 + (fb // 2 - 1) * 16)
                        a.activation(yb[:, k, :], ps[:, 6, :], ACT.Copy, scale=1.0 / WSCALE).then_inc(y_ok, 1)
                    if mode == "shared":
                        if i == 0:
                            a.wait_ge(diff_ok, 1)
                            a.activation(EX, EX, ACT.Exp).then_inc(e_ok, 1)
                        for u in units_at[i]:
                            high_part(SLAB + u // 2, u % 2)

                hi_part(0, base % 2)
                pipeline(a, base, n, step)

            router()
            a.wait_ge(st_out, 16 * 2 * NT * B)
            tiles(TT, ST, "shared")
            tiles(TT + ST, RT, "routed")
            tiles(TT + ST + RT, ST, "final")

        @block.vector
        def _(v):
            def newton(ch, mv_, nw_):
                var, half, tmp, y = (nw_[:, i, :] for i in range(4))
                ch.link(v.tensor_scalar(var, mv_[:, :, 1], EPS, None, ALU.add))
                ch.link(v.tensor_scalar(tmp.bitcast(I32), var.bitcast(I32), 1, None, ALU.arith_shift_right))
                ch.link(v.tensor_scalar(half, var, -0.5, None, ALU.mult))
                ch.link(v.tensor_scalar(y.bitcast(I32), tmp.bitcast(I32), -1, MAGIC, ALU.mult, ALU.add))
                for _ in range(3):
                    ch.link(v.tensor_tensor(tmp, y, y, ALU.mult))
                    ch.link(v.tensor_tensor(tmp, tmp, half, ALU.mult))
                    ch.link(v.scalar_tensor_tensor(out=y, in0=tmp, scalar=1.5, in1=y, op0=ALU.add, op1=ALU.mult))

            def norm_stats(ch, src, st, mv_):
                for t in range(NT):
                    ins = v.bn_stats(st[:, t, :], src[:, t, :])
                ch.link(ins, v_waits)
                for t in range(NT):
                    ins = v.bn_aggr(mv_[:, t, :], st[:, t, :])
                ch.link(ins)

            def x_chain(b):
                return Chain(v, ch_ln, b * N_LN)

            def x_stats(b, ch):
                v.wait_ge(x_in, 16 * b + 16)
                norm_stats(ch, xb, stats, mv)

            def x_divide():
                for t in range(NT):
                    v.tensor_scalar(xb[:, t, :], xb[:, t, :], mv[:, t, 0:1], nw[:, 3, t:t + 1], ALU.subtract,
                                    ALU.mult).then_inc(xn_ok, 1)

            def norm_x(b):
                ch = x_chain(b)
                x_stats(b, ch)
                newton(ch, mv, nw)
                x_divide()

            def low_parts_of_rows(b):
                for t in range(NT):
                    v.wait_ge(xhi_ok, NT * b + t + 1)
                    v.tensor_tensor(xlo[:, :, t * P:(t + 1) * P],
                                    ps[:, XT_BANK[t], :].rearrange("p (k t) -> p k t", k=KC),
                                    xhi[:, :, t * P:(t + 1) * P], ALU.subtract).then_inc(xlo_ok, 1)

            def rotate(b):
                ch = Chain(v, ch_rope, b * N_ROPE)
                wait_apart(v, vc_ok, b, v_waits)
                v.wait_ge(kst_in, 16 * 3 * KVH * b)
                v.wait_ge(qst_in, 16 * 3 * REP * b)
                for k in range(6):
                    if k < 5:
                        wait_apart(v, qb_ok, 5 * b + k + 1, v_waits)
                        exchange = v.stream_shuffle(sh, qb[:, k % 2, :], [(i + DK // 2) % DK for i in range(DK)])
                    if k >= 1:
                        c = CHUNK[k - 1]
                        v.tensor_tensor(qk_lo[:, c, :], rot, qk_hi[:, c, :], ALU.subtract).then_inc(rope_ok, 1)
                    if k < 5:
                        ch.link(exchange)
                        ch.link(v.tensor_tensor(sh, sh, sin_sb, ALU.mult))
                        v.wait_ge(t1_ok, 5 * b + k + 1)
                        v.wait_ge(rope_ok, 5 * b + k)
                        ch.link(v.tensor_tensor(rot, t1[:, k % 2, :], sh, ALU.add))
                        ch.link(v.tensor_copy(qk_hi[:, CHUNK[k], :], rot))
                v.wait_ge(rope_ok, 5 * b + 5)
                assert ch.n == N_ROPE, ch.n

            def values(b):
                for half in range(2):
                    v.wait_ge(proj_ok, 7 * b + 6 + half)
                    for i in range(2):
                        ins = v.scalar_tensor_tensor(out=Vn[:, 2 * half + i, :],
                                                     in0=ps[:, V_BANK[half], i * P:(i + 1) * P], scalar=1.0 / WSCALE,
                                                     in1=bv_sb, op0=ALU.mult, op1=ALU.add)
                    ins.then_inc(v_ok, 1)

            def maxima(b):
                for u in range(PAIRS):
                    t, hp = u // (HEADS // 2), u % (HEADS // 2)
                    v.wait_ge(pair_ok, b * (2 * PAIRS) + (u + 1))
                    if u == 0:
                        v.wait_ge(mt_ps, b)
                    bank = ROW_BANK[u % 3]
                    v.tensor_reduce(m[:, t, 2 * hp:2 * hp + 2], ps[:, bank:bank + 2, 0:P * (t + 1)],
                                    AX.X, ALU.max).then_inc(m_ok, 1)
                v.wait_ge(nmhi_ok, b + 1)
                v.scalar_tensor_tensor(out=nm_lo[0:HEADS, :], in0=ps[0:HEADS, 5, :], scalar=-1.0,
                                       in1=nm_hi[0:HEADS, :], op0=ALU.mult, op1=ALU.subtract).then_inc(nmlo_ok, 1)

            def normalise(b, c):
                v.wait_ge(pv_ok, PAIRS * b + (8 * c + 8))
                v.wait_ge(oTp_ok, KVH * b + c)
                v.reciprocal(recip, ps[:, GROUP_BANK[c] + 1, :]).then_inc(rc_ok, 1)
                v.wait_ge(rc_ok, b * (2 * KVH) + (2 * c + 1))
                v.tensor_tensor(recip, ps[:, GROUP_BANK[c], :], recip, ALU.mult).then_inc(oT_ok, 1)
                v.wait_ge(oT_ok, KVH * b + (c + 1))
                v.tensor_copy(oT_hi[:, c, :], recip).then_inc(rc_ok, 1)
                v.wait_ge(rc_ok, b * (2 * KVH) + (2 * c + 2))
                v.tensor_tensor(oT_lo[:, c, :], recip, oT_hi[:, c, :], ALU.subtract).then_inc(oTp_ok, 1)

            def context(b):
                v.wait_ge(si_ps, b + 1)
                v.wait_ge(th_ok, NT * b)
                v.tensor_scalar(sib, ps[:, 5, 0:NT], bx_sb[:, 0:1], 0.5, ALU.add, ALU.mult).then_inc(sib_ok, 1)

            def add_output(b, t):
                v.wait_ge(op_ps, NT * b + (t + 1))
                v.wait_ge(xrb_ok, NT * b + (t + 1))
                v.scalar_tensor_tensor(out=xr[:, t, :], in0=ps[:, OUT_BANK[t], :], scalar=1.0 / WSCALE,
                                       in1=xr[:, t, :], op0=ALU.mult, op1=ALU.add).then_inc(x2_ok, 1)

            def after_chain(b):
                return Chain(v, ch_op, b * N_AFTER)

            def x2_stats(b, ch):
                v.wait_ge(x2_ok, NT * b + NT)
                norm_stats(ch, xr, stats2, mv2)
                newton(ch, mv2, nw2)
                ch.link(v.tensor_tensor(lnB, mv2[:, :, 0], nw2[:, 3, :], ALU.mult))
                v.tensor_scalar(lnA, nw2[:, 3, :], 0.4, 1.0, ALU.mult, ALU.add)
                ch.link(v.tensor_scalar(lnB, lnB, -0.4, 0.3, ALU.mult, ALU.add))

            def form_x3(b, ch):
                v.wait_ge(th_ok, NT * b + NT)
                v.wait_ge(st_out, 16 * 2 * NT * b)
                for t in range(NT):
                    ch.link(v.tensor_scalar(x3s[:, t, :], xr[:, t, :], lnA[:, t:t + 1], lnB[:, t:t + 1], ALU.mult,
                                            ALU.add))
                    v.scalar_tensor_tensor(out=x3s[:, t, :], in0=th[:, t, :], scalar=0.3, in1=x3s[:, t, :],
                                           op0=ALU.mult, op1=ALU.add).then_inc(x3_ok, 1)

            def x3_stats(b, ch):
                v.wait_ge(x3_ok, NT * b + NT)
                norm_stats(ch, x3s, stats2, mv2)
                newton(ch, mv2, nw2)

            def form_h3(b, ch):
                if h3_place(b) is x3s:
                    v.wait_ge(st_out, b * (16 * 2 * NT) + 16 * NT)
                for t in range(NT):
                    v.tensor_scalar(h3_place(b)[:, t, :], x3s[:, t, :], mv2[:, t, 0:1], nw2[:, 3, t:t + 1], ALU.subtract,
                                    ALU.mult).then_inc(h3_ok, 1)
                assert ch.n == N_AFTER, ch.n

            def low_part(s, half):
                o, dst, n, _ = halves[half]
                v.wait_ge(whi_ok, s * 2 + (half + 1))
                v.scalar_tensor_tensor(out=w_cols(s * WN, dst + n, n), in0=stage[:, o:o + n], scalar=WSCALE,
                                       in1=w_cols(s * WN, dst, n), op0=ALU.mult, op1=ALU.subtract).then_inc(wlo_ok, 1)

            v.memset(Kst[96:98, :, :], 1.0).then_inc(kones_ok, 1)
            norm_x(0)
            low_parts_of_rows(0)
            v.wait_ge(wqkv_hi_ok, 1)
            v.scalar_tensor_tensor(out=wqkv_lo.rearrange("p k n -> p (k n)"), in0=stage[:, 0:KC * NQKV], scalar=WSCALE,
                                   in1=wqkv_hi.rearrange("p k n -> p (k n)"), op0=ALU.mult,
                                   op1=ALU.subtract).then_inc(wqkv_ok, 1)
            v.wait_ge(par_in, 16 * NPAR)
            rotate(0)
            values(0)
            norm_x(1)
            v.wait_ge(wo_hi_ok, 1)
            v.scalar_tensor_tensor(out=wo_lo, in0=wo_stage, scalar=WSCALE, in1=wo_hi, op0=ALU.mult,
                                   op1=ALU.subtract).then_inc(wo_ok, 1)

            def batch(b):
                maxima(b)
                if has(b, 1):
                    low_parts_of_rows(b + 1)
                    rotate(b + 1)
                    values(b + 1)
                ch = after_chain(b - 1) if has(b, -1) else None
                if ch:
                    x2_stats(b - 1, ch)
                normalise(b, 0)
                if ch:
                    form_x3(b - 1, ch)
                normalise(b, 1)
                if ch:
                    x3_stats(b - 1, ch)
                normalise(b, 2)
                normalise(b, 3)
                context(b)
                if ch:
                    form_h3(b - 1, ch)
                add_output(b, 0)
                if has(b, 2):
                    xch = x_chain(b + 2)
                    x_stats(b + 2, xch)
                add_output(b, 1)
                if has(b, 2):
                    newton(xch, mv, nw)
                add_output(b, 2)
                if has(b, 2):
                    x_divide()
                add_output(b, 3)

            batches(v, batch)
            rch = Chain(v, r_dve)
            v.wait_ge(g_in, 16)
            rch.link(v.tensor_scalar(g_f, g_f, WSCALE, None, ALU.mult))
            v.memset(ps[96:P, 5, 2 * P:3 * P], 0.0).then_inc(g_ok, 1)
            rch.link(v.tensor_copy(g_hi, g_f))
            v.tensor_tensor(g_lo, g_f, g_hi, ALU.subtract).then_inc(g_ok, 1)

            def route_tiles(first, last):
                def lo_part(i, k):
                    v.wait_ge(bhi_ok, i + 1)
                    v.tensor_tensor(blo[:, k, :, :], ps[:, 6 * k, :].rearrange("p (k t) -> p k t", k=KC), bhi[:, k, :, :],
                                    ALU.subtract).then_inc(blo_ok, 1)

                def take_logits(i, k):
                    v.wait_ge(lg_ps, i + 1)
                    v.tensor_scalar(LG[:, i, :], ps[:, 7 - 2 * k, 0:NE], 1.0 / WSCALE, None, ALU.mult).then_inc(lg_ok, 1)

                for i in range(first, last):
                    lo_part(i, i % 2)
                    if i >= 1:
                        take_logits(i - 1, (i - 1) % 2)
                if last == TT:
                    take_logits(TT - 1, 1)

            ch = after_chain(B - 1)
            route_tiles(0, NT)
            x2_stats(B - 1, ch)
            route_tiles(NT, 2 * NT)
            form_x3(B - 1, ch)
            route_tiles(2 * NT, 3 * NT)
            x3_stats(B - 1, ch)
            form_h3(B - 1, ch)
            route_tiles(3 * NT, TT)

            def best_two():
                v.wait_ge(bconst, 5)
                v.wait_ge(lg_ok, TT)
                for t in range(TT):
                    ins = v.max(srt[:, t, :], LG[:, t, :])
                rch.link(ins)
                for t in range(TT):
                    ins = v.max_index(sidx[:, t, :], srt[:, t, :], LG[:, t, :])
                rch.link(ins)
                v.tensor_tensor(EX, srt, srt[:, :, 0:1].to_broadcast([P, TT, NE]), ALU.subtract).then_inc(diff_ok, 1)
                for c in range(2):
                    rch.link(v.tensor_copy(idx_f[:, c, :], sidx[:, :, c]))
                for c, one_hot in ((0, M1), (1, M2)):
                    rch.link(v.tensor_tensor(one_hot, iota8, idx_f[:, c, :].unsqueeze(2).to_broadcast([P, TT, NE]),
                                             ALU.is_equal))
                v.tensor_tensor(Mb, M1.rearrange("p t e -> p (t e)"), M2.rearrange("p t e -> p (t e)"), ALU.add)\
                    .then_inc(mb_ok, 1)

            def count_pairs():
                v.wait_ge(cnt_ps, 1)
                tot = ps[:, 7, TT * NE:2 * TT * NE].rearrange("p (t e) -> p t e", t=TT)
                rch.link(v.memset(pre[:, 0, :], 0.0))
                for t in range(1, TT):
                    rch.link(v.tensor_tensor(pre[:, t, :], tot[:, t - 1, :], pre[:, t - 1, :], ALU.add))
                rch.link(v.tensor_tensor(nte[:, 0, :], tot[:, TT - 1, :], pre[:, TT - 1, :], ALU.add))
                rch.link(v.tensor_tensor(cmp, it128, nte[:, 0, :].unsqueeze(2).to_broadcast([P, NE, 16]), ALU.is_lt))
                rch.link(v.tensor_reduce(nte[:, 1, :], cmp, AX.X, ALU.add))
                rch.link(v.tensor_copy(nte[:, 2, 0:1], nte[:, 1, 0:1]))
                for e in range(1, NE):
                    rch.link(v.tensor_tensor(nte[:, 2, e:e + 1], nte[:, 2, e - 1:e], nte[:, 1, e:e + 1], ALU.add))

            def place_pairs():
                rch.link(v.tensor_tensor(cmt, itile, nte[:, 2:3, :].to_broadcast([P, RT, NE]), ALU.is_ge))
                rch.link(v.tensor_reduce(toff_f[:, 0:RT], cmt, AX.X, ALU.add))
                rch.link(v.tensor_scalar(toff_f[:, 0:RT], toff_f[:, 0:RT], float(NE - 1), float(WN), ALU.min, ALU.mult))
                v.tensor_scalar(toff[:, 0:RT], toff_f[:, 0:RT], float(WN), None, ALU.add).then_inc(table_ok, 1)
                rch.link(v.tensor_tensor(nte[:, 3, :], nte[:, 2, :], nte[:, 1, :], ALU.subtract))
                rch.link(v.tensor_scalar(nte[:, 3, :], nte[:, 3, :], float(P), None, ALU.mult))
                rch.link(v.tensor_tensor(R, ps[:, 7, 0:TT * NE].rearrange("p (t e) -> p t e", t=TT), pre, ALU.add))
                rch.link(v.tensor_tensor(R, R, nte[:, 3:4, :].to_broadcast([P, TT, NE]), ALU.add))
                for c, one_hot in ((0, M1), (1, M2)):
                    rch.link(v.tensor_tensor(one_hot, one_hot, R, ALU.mult))
                    rch.link(v.tensor_reduce(slot_f[:, c, :], one_hot, AX.X, ALU.add))
                v.tensor_copy(slot_i, slot_f).then_inc(route_ok, 1)

            def weigh_pairs():
                v.wait_ge(e_ok, 1)
                rch.link(v.tensor_reduce(zs[:, 0, :], EX, AX.X, ALU.add))
                rch.link(v.reciprocal(zs[:, 1, :], zs[:, 0, :]))
                for c in range(2):
                    rch.link(v.tensor_tensor(zs[:, 2 + c, :], EX[:, :, c], zs[:, 1, :], ALU.mult))
                rch.link(v.scalar_tensor_tensor(out=zs[:, 0, :], in0=zs[:, 2, :], scalar=1e-20, in1=zs[:, 3, :],
                                                op0=ALU.add, op1=ALU.add))
                rch.link(v.reciprocal(zs[:, 1, :], zs[:, 0, :]))
                for c in range(2):
                    rch.link(v.tensor_tensor(w12[:, c, :], zs[:, 2 + c, :], zs[:, 1, :], ALU.mult))


            def tiles(base, n, mode):
                fb = base - TT

                def lo_part(i, k):
                    v.wait_ge(bhi_ok, i + (base + 1))
                    v.tensor_tensor(blo[:, k, :, :], ps[:, 0, :].rearrange("p (k t) -> p k t", k=KC), bhi[:, k, :, :],
                                    ALU.subtract).then_inc(blo_ok, 1)

                def add_rows(acc, rows, t, k):
                    nonlocal added
                    for c in range(2):
                        ins = v.scalar_tensor_tensor(out=acc, in0=rows[:, k, c, :], scalar=w12[:, c, t:t + 1], in1=acc,
                                                     op0=ALU.mult, op1=ALU.add)
                        if c == 0:
                            added += 1
                            ins.then_inc(fch, 1)
                            v.wait_ge(fch, added)
                    return ins

                added = 0

                def step(i, k, h):
                    if not static(i) or i < n:
                        v.wait_ge(silu_ok, i + (fb + 1))
                        if not static(i) or i + fb >= 2:
                            v.wait_ge(at_ps, i + (fb - 1))
                        v.scalar_tensor_tensor(out=act[:, k, :], in0=ps[:, 2 + 2 * k, 0:FF], scalar=1.0 / WSCALE,
                                               in1=sil[:, k, :], op0=ALU.mult, op1=ALU.mult).then_inc(act_ok, 1)
                    if not static(i) or i + 1 < n:
                        lo_part(i + 1, 1 - k)
                    if not static(i) or 1 <= i <= n:
                        v.wait_ge(ahi_ok, i + fb)
                        v.tensor_tensor(alo[:, 1 - k, :, :], ps[:, 5, 0:3 * P].rearrange("p (k t) -> p k t", k=3),
                                        ahi[:, 1 - k, :, :], ALU.subtract).then_inc(alo_ok, 1)
                    if mode == "final" and i >= 2:
                        s, seen = i % 2, i // 2
                        v.wait_ge(xs_in[s], 16 * seen)
                        v.wait_ge(ge_in[s], 32 * seen)
                        add_rows(xs[:, s, :], ge, i - 2, s).then_inc(fx_ok, 1)
                        v.wait_ge(fx_ok, i - 1)
                        if i >= 4:
                            v.wait_ge(fin_out[s], 16 * (seen - 1))
                        v.tensor_copy(fin[:, s, :], xs[:, s, :]).then_inc(fin_ok, 1)
                        v.wait_ge(x3_in[s], 16 * (ST // 2 + seen))
                        v.wait_ge(gd_in[s], 32 * seen)
                        add_rows(x3b[:, s, :], gd, ST + i - 2, s).then_inc(x3g_ok, 1)
                        v.wait_ge(x3g_ok, i - 1)
                    if mode != "routed" and i >= 2:
                        s, seen = i % 2, i // 2
                        v.wait_ge(dn_ps, i + (fb - 1))
                        v.wait_ge(x3_in[s], 16 * seen + (16 * (ST // 2) if mode == "final" else 0))
                        if i + fb >= 4:
                            v.wait_ge(y_out[k], 16 * ((i - 2 + fb) // 2))
                        v.scalar_tensor_tensor(out=yb[:, k, :], in0=ps[:, 6, :], scalar=1.0 / WSCALE, in1=x3b[:, s, :],
                                               op0=ALU.mult, op1=ALU.add).then_inc(y_ok, 1)
                    if mode == "shared":
                        if i == 0:
                            place_pairs()
                        if i == 2:
                            weigh_pairs()
                        for u in units_at[i]:
                            low_part(SLAB + u // 2, u % 2)

                lo_part(0, base % 2)
                if mode == "shared":
                    best_two()
                    count_pairs()
                pipeline(v, base, n, step)

            v.wait_ge(st_out, 16 * 2 * NT * B)
            tiles(TT, ST, "shared")
            tiles(TT + ST, RT, "routed")
            tiles(TT + ST + RT, ST, "final")

        @block.tensor
        def _(pe):
            def project(b):
                for t in range(NT):
                    pe.wait_ge(xn_ok, NT * b + (t + 1))
                    if t < 2:
                        pe.wait_ge(v_ok, 2 * b)
                    for k in range(KC):
                        ins = pe.transpose(ps[:, XT_BANK[t], k * P:(k + 1) * P], xb[:, t, k * P:(k + 1) * P], ident[:, :])
                    ins.then_inc(xt_ok, 1)
                pe.wait_ge(xlo_ok, NT * b + 1)
                pe.wait_ge(xhi_ok, NT * b + NT)
                if static(b) and b == 0:
                    pe.wait_ge(wqkv_hi_ok, 1)
                terms = ((wqkv_hi, xhi), (wqkv_hi, xlo), (wqkv_lo, xhi))
                for k, c in enumerate(CHUNK):
                    if k >= 2:
                        pe.wait_ge(qb_ok, 5 * b + (k - 1))
                    n = 0
                    for wpart, xpart in terms:
                        if k == 0 and xpart is xlo:
                            pe.wait_ge(xlo_ok, NT * b + NT)
                        if static(b) and b == 0 and k == 0 and wpart is wqkv_lo:
                            pe.wait_ge(wqkv_ok, 1)
                        for kc in range(KC):
                            ins = pe.matmul(ps[:, PROJ_BANK[k], :], wpart[:, kc, c * P:(c + 1) * P], xpart[:, kc, :],
                                            start=(n == 0), stop=(n == 3 * KC - 1))
                            n += 1
                    ins.then_inc(proj_ok, 1)
                for half in range(2):
                    pe.wait_ge(qb_ok, 5 * b + (4 + half))
                    for i in range(2):
                        t, n = 2 * half + i, 0
                        for wpart, xpart in terms:
                            for kc in range(KC):
                                ins = pe.matmul(ps[:, V_BANK[half], i * P:(i + 1) * P], xpart[:, kc, t * P:(t + 1) * P],
                                                wpart[:, kc, D + P:NQKV], start=(n == 0), stop=(n == 3 * KC - 1))
                                n += 1
                    ins.then_inc(proj_ok, 1)

            def context(b):
                pe.wait_ge(ctx_ld, 16 * b + 16)
                pe.wait_ge(oT_ok, KVH * b + 3)
                for t in range(NT):
                    ins = pe.transpose(ps[:, 4, t * P:(t + 1) * P], ctx_sb[:, t, :], ident[:, :])
                ins.then_inc(ctxT_ps, 1)
                pe.wait_ge(ctxT_ok, b + 1)
                for t in range(NT):
                    ins = pe.matmul(ps[:, 5, t:t + 1], ctxT[:, t * P:(t + 1) * P], wi_sb[:, 0:1], start=True, stop=True)
                ins.then_inc(si_ps, 1)
                pe.matmul(ps[:, 4, :], wj_sb, ctxT, start=True, stop=True).then_inc(sj_ps, 1)

            def row_scores(b):
                pe.wait_ge(kst_in, 16 * 3 * KVH * b + 16 * 3 * KVH)
                pe.wait_ge(qst_in, 16 * 3 * REP * b + 16 * 3 * REP)
                for u in range(PAIRS):
                    t, hp = u // (HEADS // 2), u % (HEADS // 2)
                    if u < 2:
                        pe.wait_ge(p_ok, PAIRS * b)
                    elif u == 2:
                        pe.wait_ge(x2_ok, NT * b)
                        pe.wait_ge(v_ok, 2 * b + 2)
                    else:
                        pe.wait_ge(m_ok, PAIRS * b + (u - 2))
                    for i in range(2):
                        h = 2 * hp + i
                        bank = ROW_BANK[u % 3] + i
                        o = ps[:, bank, 0:P * (t + 1)]
                        pe.matmul(o, Qst[0:96, h, t * P:(t + 1) * P], Kst[0:96, h // REP, 0:P * (t + 1)],
                                  start=True, stop=False)
                        ins = pe.matmul(ps[:, bank, P * t:P * (t + 1)], identb, mk, start=False, stop=True)
                    ins.then_inc(pair_ok, 1)
                pe.wait_ge(m_ok, PAIRS * b + PAIRS)
                pe.wait_ge(x2_ok, NT * b)
                for t in range(NT):
                    ins = pe.transpose(ps[0:HEADS, 5, t * P:(t + 1) * P], m[:, t, :], ident[:, :])
                ins.then_inc(mt_ps, 1)

            def attend(b):
                LAG = 2

                def products(u):
                    c, j, r2 = u // 8, u // 2 % NT, u % 2
                    n = T - P * j
                    pe.wait_ge(mask_ok, PAIRS * b + (u + 1))
                    if u % 8 == 0:
                        if c == 0:
                            pe.wait_ge(vc_ok, b + 1)
                            pe.wait_ge(th_ok, NT * b)
                            pe.wait_ge(nmlo_ok, b + 1)
                        elif c == 1:
                            if has(b, 1):
                                pe.wait_ge(v_ok, 2 * b + 4)
                        else:
                            pe.wait_ge(oT_ok, KVH * b + (c - 1))
                    for bank, left in ((GROUP_BANK[c], V[:, j, c * DK:(c + 1) * DK]), (GROUP_BANK[c] + 1, ones32)):
                        for i in range(2):
                            r = 2 * r2 + i
                            ins = pe.matmul(ps[r * DK:(r + 1) * DK, bank, P * j:T], left, pT[:, u % 4, i, 0:n],
                                            start=(j == 0), stop=(j == NT - 1), tile_position=(0, r * DK))
                    ins.then_inc(pv_ok, 1)

                pe.wait_ge(nm_in, 32 * b + 32)
                for u in range(PAIRS + LAG):
                    if u < PAIRS:
                        c, j, r2 = u // 8, u // 2 % NT, u % 2
                        if u < 2:
                            pe.wait_ge(m_ok, PAIRS * b + PAIRS)
                        else:
                            pe.wait_ge(p_ok, PAIRS * b + (u - 1))
                        for i in range(2):
                            ins = pe.matmul(ps[:, 2 * (u % 2) + i, 0:T - P * j], Kst[0:98, c, P * j:P * (j + 1)],
                                            Qst[0:98, REP * c + 2 * r2 + i, P * j:T], start=True, stop=True)
                        ins.then_inc(pair_ok, 1)
                    if u >= LAG:
                        products(u - LAG)

            def output(b):
                pe.wait_ge(oTp_ok, KVH * b + KVH)
                pe.wait_ge(sib_ok, b + 1)
                if static(b) and b == 0:
                    pe.wait_ge(wo_ok, 1)
                for t in range(NT):
                    if t >= 2:
                        pe.wait_ge(x2_ok, NT * b + (t - 1))
                    n = 0
                    for opart, wpart in ((oT_hi, wo_hi), (oT_hi, wo_lo), (oT_lo, wo_hi)):
                        for c in range(KC):
                            ins = pe.matmul(ps[:, OUT_BANK[t], :], opart[:, c, t * P:(t + 1) * P], wpart[:, c, :],
                                            start=(n == 0), stop=(n == 3 * KC - 1))
                            n += 1
                    ins.then_inc(op_ps, 1)

            pe.wait_ge(consts_ok, 4)
            pe.wait_ge(kones_ok, 1)
            project(0)
            pe.wait_ge(par_in, 16 * NPAR)

            def batch(b):
                row_scores(b)
                if has(b, 1):
                    project(b + 1)
                attend(b)
                context(b)
                output(b)

            batches(pe, batch)

            def router():
                def transpose_rows(i, k):
                    own = i >= (B - 1) * NT
                    if own:
                        pe.wait_ge(h3_ok, i + 1)
                    else:
                        pe.wait_ge(row_in[i // NT], 16)
                    if i >= 2:
                        pe.wait_ge(blo_ok, i - 1)
                    for c in range(KC):
                        row = (xr[:, i % NT, :] if own else rows16[:, i, :])[:, c * P:(c + 1) * P]
                        ins = pe.transpose(ps[:, 6 * k, c * P:(c + 1) * P], row, ident[:, :])
                    ins.then_inc(bt_ps, 1)

                def logits(i, k):
                    pe.wait_ge(blo_ok, i + 1)
                    if i >= 2:
                        pe.wait_ge(lg_ok, i - 1)
                    n = 0
                    for left, g in ((bhi, g_hi), (bhi, g_lo), (blo, g_hi)):
                        for c in range(KC):
                            ins = pe.matmul(ps[:, 7 - 2 * k, 0:NE], left[:, k, c, :], g[:, c, :], start=(n == 0),
                                            stop=(n == 3 * KC - 1))
                            n += 1
                    ins.then_inc(lg_ps, 1)

                for i in range(TT + 1):
                    if i < TT:
                        transpose_rows(i, i % 2)
                    if i >= 1:
                        logits(i - 1, (i - 1) % 2)

            def tiles(base, n, mode):
                fb = base - TT

                def transpose_rows(i, k, h):
                    pe.wait_ge(b_in[k], 16 * ((i + fb) // 2 + 1) if static(i) else h * 16 + (fb // 2 + 1) * 16)
                    pe.wait_ge(blo_ok, i + base)
                    for c in range(KC):
                        ins = pe.transpose(ps[:, 0, c * P:(c + 1) * P], bx[:, k, c * P:(c + 1) * P], ident[:, :])
                    ins.then_inc(bt_ps, 1)

                def expert_of(i):
                    if mode != "routed":
                        return 0
                    at = toff[0:1, i:i + 1] if static(i) else toff[0:1, bass.ds(i, 1)]
                    return pe.value_load(at, min_val=WN, max_val=NE * WN)

                def up(i, k):
                    off = expert_of(i)
                    pe.wait_ge(blo_ok, i + (base + 1))
                    if not static(i) or i + fb >= 2:
                        pe.wait_ge(act_ok, i + (fb - 1))
                    n = 0
                    for left, part in ((bhi, 0), (bhi, 1), (blo, 0)):
                        for c in range(KC):
                            for g in range(2):
                                ins = pe.matmul(ps[:, 1 + 2 * k + g, 0:FF], left[:, k, c, :],
                                                w_cols(off, part * W1N + c * 2 * FF + g * FF, FF),
                                                start=(n == 0), stop=(n == 3 * KC - 1))
                            n += 1
                    ins.then_inc(up_ps, 1)

                def down(i, k):
                    off = expert_of(i)
                    pe.wait_ge(alo_ok, i + (fb + 1))
                    pe.wait_ge(y_ok, i + fb)
                    n = 0
                    for left, part in ((ahi, 0), (ahi, 1), (alo, 0)):
                        for c, (_, r) in enumerate(FCH):
                            ins = pe.matmul(ps[:, 6, :], left[0:r, k, c, :],
                                            w_cols(off, 2 * W1N + part * W2N + c * D, D, r), start=(n == 0), stop=(n == 8))
                            n += 1
                    ins.then_inc(dn_ps, 1)

                def step(i, k, h):
                    if not static(i) or i < n:
                        up(i, k)
                    if not static(i) or i + 1 < n:
                        transpose_rows(i + 1, 1 - k, h + i % 2 if static(i) else h + k)
                    if not static(i) or 1 <= i <= n:
                        pe.wait_ge(act_ok, i + fb)
                        if not static(i) or i + fb >= 2:
                            pe.wait_ge(alo_ok, i + (fb - 1))
                        for c, (o, r) in enumerate(FCH):
                            ins = pe.transpose(ps[0:r, 5, c * P:(c + 1) * P], act[:, 1 - k, o:o + r], ident[:, :])
                        ins.then_inc(at_ps, 1)
                    if not static(i) or i >= 2:
                        down(i - 2, k)
                transpose_rows(0, base % 2, 0)
                if mode == "shared":
                    pe.wait_ge(mb_ok, 1)
                    pe.wait_ge(lg_ok, TT)
                    pe.matmul(ps[:, 7, 0:TT * NE], lt_b, Mb, start=True, stop=True)
                    pe.matmul(ps[:, 7, TT * NE:2 * TT * NE], on_b, Mb, start=True, stop=True).then_inc(cnt_ps, 1)
                pipeline(pe, base, n, step)

            pe.wait_ge(x2_ok, NT * B)
            pe.wait_ge(g_ok, 2)
            router()
            pe.wait_ge(wlo_ok, 2)
            tiles(TT, ST, "shared")
            pe.wait_ge(wlo_ok, 2 * (NE + 1))
            pe.wait_ge(table_ok, 1)
            pe.wait_ge(route_ok, 1)
            tiles(TT + ST, RT, "routed")
            tiles(TT + ST + RT, ST, "final")


def rope_tables():
    import numpy as np
    half = DK // 2
    inv = (1.0 / 10000.0 ** (np.arange(half, dtype=np.float32) / np.float32(half))).astype(np.float32)
    ang = np.arange(T, dtype=np.float32)[None, :] * inv[:, None]
    cos, sin = np.cos(ang).astype(np.float32), np.sin(ang).astype(np.float32)
    return (np.ascontiguousarray(np.tile(np.concatenate([cos, cos]), (P // DK, 1))),
            np.ascontiguousarray(np.tile(np.concatenate([-sin, sin]), (P // DK, 1))))


def kernel(**inputs):
    import numpy as np
    import concourse.bacc as bacc
    from concourse import mybir as mb
    from concourse.bass_utils import run_bass_kernel_spmd

    nc = bacc.Bacc("TRN2", target_bir_lowering=False, num_devices=1)
    g = {k: np.asarray(v) for k, v in inputs.items()}
    cosT, sinT = rope_tables()
    W12 = g["L0_xattn_W"]
    w1 = np.concatenate([np.concatenate([g["L0_ffn_sw1"].T, g["L0_ffn_sw2"].T], axis=1)[None], g["L0_ffn_w1"]])
    w2 = np.concatenate([g["L0_ffn_sw3"].T[None], g["L0_ffn_w2"]])
    w2 = np.concatenate([w2, np.zeros((NE + 1, len(FCH) * P - FF, D), np.float32)], axis=1)
    ins = {
        "x": g["x"], "ctx": g["ctx_512"], "wq": g["L0_attn_wq_w"], "wk": g["L0_attn_wk_w"], "wv": g["L0_attn_wv_w"],
        "bqk": np.concatenate([g["L0_attn_wq_b"], g["L0_attn_wk_b"]]).reshape(5, P).T,
        "bv": np.broadcast_to(g["L0_attn_wv_b"], (P, P)),
        "wo": g["L0_attn_o_w"], "bo": np.broadcast_to(g["L0_attn_o_b"], (P, D)),
        "wi": W12[0, :CTX].reshape(CTX, 1), "wj": np.broadcast_to(W12[0, CTX:].reshape(CTX, 1), (CTX, P)),
        "b_x": np.broadcast_to(g["L0_xattn_b"], (P, 1)), "gate": g["L0_ffn_gate_w"].T,
        "w1": w1, "w2": w2, "cosT": cosT, "sinT": sinT,
    }
    arrays, aps = {}, {}
    for name, a in ins.items():
        a = np.ascontiguousarray(a)
        arrays["in_" + name] = a
        aps[name] = nc.dram_tensor("in_" + name, a.shape, mb.dt.float32, kind="ExternalInput").ap()
    aps["out"] = nc.dram_tensor("out_0", (B, T, D), mb.dt.float32, kind="ExternalOutput").ap()
    for name, n in (("h3d", TOK), ("xsd", TOK), ("x3d", TOK), ("disp", RT * P), ("yd", RT * P)):
        aps[name] = nc.dram_tensor(name, (n, D), mb.dt.float32).ap()
    decoder_kernel(nc, **aps)
    r = run_bass_kernel_spmd(nc, [arrays], core_ids=[0])
    return r.results[0]["out_0"]
```
